# Optimizing a Trainium2 kernel written in Bass

```python
import numpy as np
import jax
import jax.numpy as jnp

def _softmax(x, axis=-1):
    return jax.nn.softmax(x, axis=axis)

def _gelu(x):
    return jax.nn.gelu(x, approximate=True)

def _silu(x):
    return jax.nn.silu(x)

def _sigmoid(x):
    return jax.nn.sigmoid(x)

def _layernorm(x, axis=-1, eps=1e-05):
    m = jnp.mean(x, axis=axis, keepdims=True)
    v = jnp.var(x, axis=axis, keepdims=True)
    return (x - m) / jnp.sqrt(v + eps)

def _scatter_add(tgt, idx, src, axis=0):
    return tgt.at[idx].add(src)

def _segment_sum(src, seg, n):
    return jax.ops.segment_sum(src, seg, n)
kernel_name = 'mk_xattn_seq_d2_seqx_r8_ca9556'

def setup_inputs(seed: int=0):
    np.random.seed(seed)
    _w = jnp.asarray

    def _rec_inputs():
        import jax
        import jax.numpy as jnp
        _rk = jax.random.key(seed)
        x = -0.0002928 + 1 * jax.random.normal(jax.random.fold_in(_rk, 1), (8, 128, 256), jnp.float32)
        _lenS = 128 - jax.random.randint(jax.random.fold_in(_rk, 7), (8,), 0, max(1, 128 // 4) + 1, jnp.int32)
        _lenS2 = 128 - jax.random.randint(jax.random.fold_in(_rk, 8), (8,), 0, max(1, 128 // 4) + 1, jnp.int32)
        _ctx_2048P = jax.random.normal(jax.random.fold_in(_rk, 11), (8, 16, 256), jnp.float32)
        _ctx_2048c = jax.random.dirichlet(jax.random.fold_in(_rk, 511), 0.3 * jnp.ones((16,), jnp.float32), (8, 128))
        _ctx_2048t = jnp.einsum('bsk,bkd->bsd', _ctx_2048c, _ctx_2048P)
        _ctx_2048t = _ctx_2048t * jax.lax.rsqrt(jnp.mean(jnp.square(_ctx_2048t)) + 1e-12) * 0.953939
        ctx_2048 = -1.39393e-06 + 0.999914 * (_ctx_2048t + 0.3 * jax.random.normal(jax.random.fold_in(_rk, 611), (8, 128, 256), jnp.float32))
        return (x, ctx_2048)
    x, ctx_2048 = _rec_inputs()

    def _L0_xattn_setup():
        import math
        import jax, jax.numpy as jnp
        import numpy as np
        C = 128
        H = 16
        DH = C // H
        EPS = 1e-05

        def pos_enc(c, T, dtype):
            pos = jnp.arange(T, dtype=jnp.float32)[:, None]
            div = jnp.exp(jnp.arange(0, c, 2, dtype=jnp.float32) * (-math.log(10000.0) / c))
            ang = pos * div
            pe = jnp.zeros((T, c), dtype=jnp.float32)
            pe = pe.at[:, 0::2].set(jnp.sin(ang)).at[:, 1::2].set(jnp.cos(ang))
            return pe.T.astype(dtype)

        def layer_norm(x, g, b):
            mu = jnp.mean(x, axis=-1, keepdims=True)
            var = jnp.mean(jnp.square(x - mu), axis=-1, keepdims=True)
            return (x - mu) * jax.lax.rsqrt(var + EPS) * g + b
        key = jax.random.key(seed)
        ks = jax.random.split(key, 16)
        s = 1.0 / math.sqrt(C)
        inp = {'zt_prev': jax.random.normal(ks[0], (2, C, 256), jnp.float32), 'za': jax.random.normal(ks[1], (2, C, 256), jnp.float32), 'Wq': jax.random.normal(ks[2], (C, C), jnp.float32) * s, 'Wk': jax.random.normal(ks[3], (C, C), jnp.float32) * s, 'Wv': jax.random.normal(ks[4], (C, C), jnp.float32) * s, 'Wo': jax.random.normal(ks[5], (C, C), jnp.float32) * s, 'ln_q_g': jnp.ones((C,), jnp.float32), 'ln_q_b': jnp.zeros((C,), jnp.float32), 'ln_kv_g': jnp.ones((C,), jnp.float32), 'ln_kv_b': jnp.zeros((C,), jnp.float32), 'ffn_ln_g': jnp.ones((C,), jnp.float32), 'ffn_ln_b': jnp.zeros((C,), jnp.float32), 'W1': jax.random.normal(ks[6], (C, 2 * C), jnp.float32) * s, 'b1': jnp.zeros((2 * C,), jnp.float32), 'W2': jax.random.normal(ks[7], (2 * C, C), jnp.float32) * (1.0 / math.sqrt(2 * C)), 'b2': jnp.zeros((C,), jnp.float32)}
        return inp
    _L0_xattn_all = _L0_xattn_setup()
    _L0_xattn_in = {k: v for k, v in _L0_xattn_all.items() if k in ('Wq', 'Wk', 'Wv', 'Wo', 'ln_q_g', 'ln_q_b', 'ln_kv_g', 'ln_kv_b', 'ffn_ln_g', 'ffn_ln_b', 'W1', 'b1', 'W2', 'b2')}
    del _L0_xattn_all

    def _L1_xattn_setup():
        import jax, jax.numpy as jnp
        import numpy as np
        B, L, E, H = (4, 64, 256, 32)
        S = E // H
        EXTRA_MAA, EXTRA_DECAY = (32, 64)
        EPS = 1e-05

        def _ln(x, w, b):
            m = jnp.mean(x, axis=-1, keepdims=True)
            v = jnp.mean((x - m) ** 2, axis=-1, keepdims=True)
            return (x - m) * jax.lax.rsqrt(v + EPS) * w + b

        def _token_shift(xn, prev_row):
            first = (prev_row - xn[:, 0])[:, None]
            rest = xn[:, :-1] - xn[:, 1:]
            return jnp.concatenate([first, rest], axis=1)
        key = jax.random.key(seed)
        ks = jax.random.split(key, 24)
        rn = lambda k, shp, s=1.0: jax.random.normal(k, shp, dtype=jnp.float32) * s
        return dict(x=rn(ks[0], (B, L, E)), state=rn(ks[1], (B, 2 + S, E), 0.1), ln1_w=jnp.ones((E,), jnp.float32), ln1_b=jnp.zeros((E,), jnp.float32), ln2_w=jnp.ones((E,), jnp.float32), ln2_b=jnp.zeros((E,), jnp.float32), maa_x=rn(ks[2], (E,), 0.02), maa_w1=rn(ks[3], (E, 5 * EXTRA_MAA), 0.02), maa_w2=rn(ks[4], (5, EXTRA_MAA, E), 0.02), maa_stack=rn(ks[5], (5, E), 0.02), time_decay=rn(ks[6], (E,), 0.5), decay_w1=rn(ks[7], (E, EXTRA_DECAY), 0.02), decay_w2=rn(ks[8], (EXTRA_DECAY, E), 0.02), faaaa=rn(ks[9], (H, S), 0.1), Wr=rn(ks[10], (E, E), 0.02), Wk=rn(ks[11], (E, E), 0.02), Wv=rn(ks[12], (E, E), 0.02), Wg=rn(ks[13], (E, E), 0.02), Wo=rn(ks[14], (E, E), 0.02), gn_w=jnp.ones((E,), jnp.float32), gn_b=jnp.zeros((E,), jnp.float32), ffn_maa_k=rn(ks[15], (E,), 0.02), ffn_maa_r=rn(ks[16], (E,), 0.02), ffn_Wk=rn(ks[17], (E, E), 0.02), ffn_Wr=rn(ks[18], (E, E), 0.02), ffn_Wv=rn(ks[19], (E, E), 0.02), i=0)
    _L1_xattn_all = _L1_xattn_setup()
    _L1_xattn_in = {k: v for k, v in _L1_xattn_all.items() if k in ('ln1_w', 'ln1_b', 'ln2_w', 'ln2_b', 'maa_x', 'maa_w1', 'maa_w2', 'maa_stack', 'time_decay', 'decay_w1', 'decay_w2', 'faaaa', 'Wr', 'Wk', 'Wv', 'Wg', 'Wo', 'gn_w', 'gn_b', 'ffn_maa_k', 'ffn_maa_r', 'ffn_Wk', 'ffn_Wr', 'ffn_Wv')}
    del _L1_xattn_all
    return {'x': x, 'ctx_2048': ctx_2048, 'L0_xattn_Wq': _L0_xattn_in['Wq'], 'L0_xattn_Wk': _L0_xattn_in['Wk'], 'L0_xattn_Wv': _L0_xattn_in['Wv'], 'L0_xattn_Wo': _L0_xattn_in['Wo'], 'L0_xattn_ln_q_g': _L0_xattn_in['ln_q_g'], 'L0_xattn_ln_q_b': _L0_xattn_in['ln_q_b'], 'L0_xattn_ln_kv_g': _L0_xattn_in['ln_kv_g'], 'L0_xattn_ln_kv_b': _L0_xattn_in['ln_kv_b'], 'L0_xattn_ffn_ln_g': _L0_xattn_in['ffn_ln_g'], 'L0_xattn_ffn_ln_b': _L0_xattn_in['ffn_ln_b'], 'L0_xattn_W1': _L0_xattn_in['W1'], 'L0_xattn_b1': _L0_xattn_in['b1'], 'L0_xattn_W2': _L0_xattn_in['W2'], 'L0_xattn_b2': _L0_xattn_in['b2'], 'L1_xattn_ln1_w': _L1_xattn_in['ln1_w'], 'L1_xattn_ln1_b': _L1_xattn_in['ln1_b'], 'L1_xattn_ln2_w': _L1_xattn_in['ln2_w'], 'L1_xattn_ln2_b': _L1_xattn_in['ln2_b'], 'L1_xattn_maa_x': _L1_xattn_in['maa_x'], 'L1_xattn_maa_w1': _L1_xattn_in['maa_w1'], 'L1_xattn_maa_w2': _L1_xattn_in['maa_w2'], 'L1_xattn_maa_stack': _L1_xattn_in['maa_stack'], 'L1_xattn_time_decay': _L1_xattn_in['time_decay'], 'L1_xattn_decay_w1': _L1_xattn_in['decay_w1'], 'L1_xattn_decay_w2': _L1_xattn_in['decay_w2'], 'L1_xattn_faaaa': _L1_xattn_in['faaaa'], 'L1_xattn_Wr': _L1_xattn_in['Wr'], 'L1_xattn_Wk': _L1_xattn_in['Wk'], 'L1_xattn_Wv': _L1_xattn_in['Wv'], 'L1_xattn_Wg': _L1_xattn_in['Wg'], 'L1_xattn_Wo': _L1_xattn_in['Wo'], 'L1_xattn_gn_w': _L1_xattn_in['gn_w'], 'L1_xattn_gn_b': _L1_xattn_in['gn_b'], 'L1_xattn_ffn_maa_k': _L1_xattn_in['ffn_maa_k'], 'L1_xattn_ffn_maa_r': _L1_xattn_in['ffn_maa_r'], 'L1_xattn_ffn_Wk': _L1_xattn_in['ffn_Wk'], 'L1_xattn_ffn_Wr': _L1_xattn_in['ffn_Wr'], 'L1_xattn_ffn_Wv': _L1_xattn_in['ffn_Wv']}

def reference(x, ctx_2048, L0_xattn_Wq, L0_xattn_Wk, L0_xattn_Wv, L0_xattn_Wo, L0_xattn_ln_q_g, L0_xattn_ln_q_b, L0_xattn_ln_kv_g, L0_xattn_ln_kv_b, L0_xattn_ffn_ln_g, L0_xattn_ffn_ln_b, L0_xattn_W1, L0_xattn_b1, L0_xattn_W2, L0_xattn_b2, L1_xattn_ln1_w, L1_xattn_ln1_b, L1_xattn_ln2_w, L1_xattn_ln2_b, L1_xattn_maa_x, L1_xattn_maa_w1, L1_xattn_maa_w2, L1_xattn_maa_stack, L1_xattn_time_decay, L1_xattn_decay_w1, L1_xattn_decay_w2, L1_xattn_faaaa, L1_xattn_Wr, L1_xattn_Wk, L1_xattn_Wv, L1_xattn_Wg, L1_xattn_Wo, L1_xattn_gn_w, L1_xattn_gn_b, L1_xattn_ffn_maa_k, L1_xattn_ffn_maa_r, L1_xattn_ffn_Wk, L1_xattn_ffn_Wr, L1_xattn_ffn_Wv):
    import jax
    import jax.numpy as jnp

    def _L0_xattn_ref(zt_prev, za, Wq, Wk, Wv, Wo, ln_q_g, ln_q_b, ln_kv_g, ln_kv_b, ffn_ln_g, ffn_ln_b, W1, b1, W2, b2):
        import math
        import jax, jax.numpy as jnp
        import numpy as np
        C = 128
        H = 16
        DH = C // H
        EPS = 1e-05

        def pos_enc(c, T, dtype):
            pos = jnp.arange(T, dtype=jnp.float32)[:, None]
            div = jnp.exp(jnp.arange(0, c, 2, dtype=jnp.float32) * (-math.log(10000.0) / c))
            ang = pos * div
            pe = jnp.zeros((T, c), dtype=jnp.float32)
            pe = pe.at[:, 0::2].set(jnp.sin(ang)).at[:, 1::2].set(jnp.cos(ang))
            return pe.T.astype(dtype)

        def layer_norm(x, g, b):
            mu = jnp.mean(x, axis=-1, keepdims=True)
            var = jnp.mean(jnp.square(x - mu), axis=-1, keepdims=True)
            return (x - mu) * jax.lax.rsqrt(var + EPS) * g + b
        B, _, Tq = zt_prev.shape
        Tk = za.shape[-1]
        q = jnp.transpose(zt_prev + pos_enc(C, Tq, zt_prev.dtype)[None], (0, 2, 1))
        kv = jnp.transpose(za + pos_enc(C, Tk, za.dtype)[None], (0, 2, 1))
        q = layer_norm(q, ln_q_g, ln_q_b)
        kv = layer_norm(kv, ln_kv_g, ln_kv_b)

        def split(x):
            Bt, T, _ = x.shape
            return jnp.transpose(x.reshape(Bt, T, H, DH), (0, 2, 1, 3))
        Q = split(q @ Wq)
        K = split(kv @ Wk)
        V = split(kv @ Wv)
        attn = jnp.einsum('bhqd,bhkd->bhqk', Q, K) / math.sqrt(DH)
        ctx = jnp.einsum('bhqk,bhkd->bhqd', jax.nn.softmax(attn, axis=-1), V)
        ctx = jnp.transpose(ctx, (0, 2, 1, 3)).reshape(B, Tq, C)
        y = ctx @ Wo
        r = y + q
        h = layer_norm(r, ffn_ln_g, ffn_ln_b)
        h = jax.nn.gelu(h @ W1 + b1, approximate=False) @ W2 + b2
        out = h + r
        return jnp.transpose(out, (0, 2, 1))

    def _L1_xattn_ref(x, state, ln1_w, ln1_b, ln2_w, ln2_b, maa_x, maa_w1, maa_w2, maa_stack, time_decay, decay_w1, decay_w2, faaaa, Wr, Wk, Wv, Wg, Wo, gn_w, gn_b, ffn_maa_k, ffn_maa_r, ffn_Wk, ffn_Wr, ffn_Wv, i):
        import jax, jax.numpy as jnp
        import numpy as np
        B, L, E, H = (4, 64, 256, 32)
        S = E // H
        EXTRA_MAA, EXTRA_DECAY = (32, 64)
        EPS = 1e-05

        def _ln(x, w, b):
            m = jnp.mean(x, axis=-1, keepdims=True)
            v = jnp.mean((x - m) ** 2, axis=-1, keepdims=True)
            return (x - m) * jax.lax.rsqrt(v + EPS) * w + b

        def _token_shift(xn, prev_row):
            first = (prev_row - xn[:, 0])[:, None]
            rest = xn[:, :-1] - xn[:, 1:]
            return jnp.concatenate([first, rest], axis=1)
        b, l = (x.shape[0], x.shape[1])
        i0 = (2 + S) * i + 0
        i1 = (2 + S) * i + 1
        xn = _ln(x, ln1_w, ln1_b)
        sx = _token_shift(xn, state[:, i1])
        xxx = jnp.tanh((xn + sx * maa_x) @ maa_w1).reshape(b, l, 5, 1, EXTRA_MAA)
        xxx = jnp.matmul(xxx, maa_w2).reshape(b, l, 5, E)
        x5 = xn[:, :, None] + sx[:, :, None] * (maa_stack + xxx)
        w = jnp.exp(-jnp.exp(time_decay + jnp.tanh(x5[:, :, 1] @ decay_w1) @ decay_w2))
        w = w.reshape(b, l, H, S)
        r = (x5[:, :, 3] @ Wr.T).reshape(b, l, H, S)
        k = (x5[:, :, 0] @ Wk.T).reshape(b, l, H, S)
        v = (x5[:, :, 2] @ Wv.T).reshape(b, l, H, S)
        g = jax.nn.silu(x5[:, :, 4] @ Wg.T)
        s0 = state[:, (2 + S) * i + 2:(2 + S) * (i + 1)].reshape(b, H, S, S)
        u = faaaa[None, :, :, None]

        def step(s, rkvw):
            r_t, k_t, v_t, w_t = rkvw
            a = k_t[:, :, :, None] * v_t[:, :, None, :]
            out = jnp.einsum('bhk,bhkd->bhd', r_t, u * a + s)
            return (a + w_t[:, :, :, None] * s, out)
        xs = tuple((jnp.moveaxis(t, 1, 0) for t in (r, k, v, w)))
        _, outs = jax.lax.scan(step, s0, xs)
        att = jnp.moveaxis(outs, 0, 1).reshape(b, l, E)
        a4 = att.reshape(b, l, H, S)
        m = jnp.mean(a4, axis=-1, keepdims=True)
        var = jnp.mean((a4 - m) ** 2, axis=-1, keepdims=True)
        att = ((a4 - m) * jax.lax.rsqrt(var + EPS)).reshape(b, l, E) * gn_w + gn_b
        x = x + att * g @ Wo.T
        xn2 = _ln(x, ln2_w, ln2_b)
        sx2 = _token_shift(xn2, state[:, i0])
        xk = xn2 + sx2 * ffn_maa_k
        xr = xn2 + sx2 * ffn_maa_r
        rr = jax.nn.sigmoid(xr @ ffn_Wr.T)
        kk = jnp.square(jax.nn.relu(xk @ ffn_Wk.T))
        x = x + rr * (kk @ ffn_Wv.T)
        return x
    x = _L0_xattn_ref(x, ctx_2048, L0_xattn_Wq, L0_xattn_Wk, L0_xattn_Wv, L0_xattn_Wo, L0_xattn_ln_q_g, L0_xattn_ln_q_b, L0_xattn_ln_kv_g, L0_xattn_ln_kv_b, L0_xattn_ffn_ln_g, L0_xattn_ffn_ln_b, L0_xattn_W1, L0_xattn_b1, L0_xattn_W2, L0_xattn_b2)
    x = _L1_xattn_ref(x, ctx_2048, L1_xattn_ln1_w, L1_xattn_ln1_b, L1_xattn_ln2_w, L1_xattn_ln2_b, L1_xattn_maa_x, L1_xattn_maa_w1, L1_xattn_maa_w2, L1_xattn_maa_stack, L1_xattn_time_decay, L1_xattn_decay_w1, L1_xattn_decay_w2, L1_xattn_faaaa, L1_xattn_Wr, L1_xattn_Wk, L1_xattn_Wv, L1_xattn_Wg, L1_xattn_Wo, L1_xattn_gn_w, L1_xattn_gn_b, L1_xattn_ffn_maa_k, L1_xattn_ffn_maa_r, L1_xattn_ffn_Wk, L1_xattn_ffn_Wr, L1_xattn_ffn_Wv, 0)
    return x

_drawn_inputs = setup_inputs


def setup_inputs(seed=0):
    import zlib

    import numpy as np

    out = dict(_drawn_inputs(seed))
    spreads = {'L0_xattn_ln_q_g': (1.0, 0.2),
     'L0_xattn_ln_q_b': (0.0, 0.1),
     'L0_xattn_ln_kv_g': (1.0, 0.2),
     'L0_xattn_ln_kv_b': (0.0, 0.1),
     'L0_xattn_ffn_ln_g': (1.0, 0.2),
     'L0_xattn_ffn_ln_b': (0.0, 0.1),
     'L0_xattn_b1': (0.0, 0.1),
     'L0_xattn_b2': (0.0, 0.285),
     'L1_xattn_ln1_w': (1.0, 0.6),
     'L1_xattn_ln1_b': (0.0, 0.722),
     'L1_xattn_ln2_w': (1.0, 0.6),
     'L1_xattn_ln2_b': (0.0, 0.8),
     'L1_xattn_gn_w': (1.0, 0.6),
     'L1_xattn_gn_b': (0.0, 0.8)}
    factors = {'L1_xattn_maa_x': 8.0,
     'L1_xattn_maa_w1': 8.0,
     'L1_xattn_maa_w2': 8.0,
     'L1_xattn_maa_stack': 8.0,
     'L1_xattn_time_decay': 3.641,
     'L1_xattn_decay_w1': 8.0,
     'L1_xattn_decay_w2': 8.0,
     'L1_xattn_faaaa': 7.676,
     'L1_xattn_ffn_maa_k': 8.0,
     'L1_xattn_ffn_maa_r': 8.0,
     'L1_xattn_ffn_Wk': 3.675,
     'L1_xattn_ffn_Wr': 8.0,
     'L1_xattn_ffn_Wv': 3.362}
    for name, (base, spread) in spreads.items():
        noise = np.random.default_rng([zlib.crc32(name.encode()), seed]).standard_normal(out[name].shape)
        drawn = base * np.exp(spread * noise) if base else spread * noise
        out[name] = jnp.asarray(drawn.astype(out[name].dtype))
    for name, factor in factors.items():
        out[name] = (out[name] * factor).astype(out[name].dtype)
    return out
```

```python
from contextlib import ExitStack
import math

import numpy as np
import concourse.bass as bass
from concourse import mybir

F32 = mybir.dt.float32
BF16 = mybir.dt.bfloat16
ALU = mybir.AluOpType
ACT = mybir.ActivationFunctionType
AX = mybir.AxisListType

B, C, T = 8, 128, 256
H0, D0 = 16, 8
NT = C
E = T
H1, S1 = 32, 8
NM = 32
ND = 64
EPS = 1e-5
UNROLL = 2
SCORE_SCALE = 1.0 / math.sqrt(D0)
Q_PARTS = (0, 0, 1, 1, 0, 2)
K_PARTS = (0, 1, 0, 1, 2, 0)
SCORE_ROWS = len(Q_PARTS) * D0
GUARD_ROWS = SCORE_ROWS + 2
MIX_K, MIX_W, MIX_V, MIX_R, MIX_G = range(5)

VEC_NAMES = ["ln_q_g", "ln_q_b", "ln_kv_g", "ln_kv_b", "ffn_g", "ffn_b", "b1_0", "b1_1", "b2"]
VEC_NAMES += [f"{n}_{h}" for n in ("ln1_w", "ln1_b", "ln2_w", "ln2_b", "maa_x", "stack0", "stack1", "stack2", "stack3",
                                   "stack4", "decay", "faaaa", "gn_w", "gn_b", "ffn_k", "ffn_r") for h in range(2)]
VEC = {n: j for j, n in enumerate(VEC_NAMES)}
NVEC = len(VEC_NAMES)

WEIGHTS = [("center", C), ("ident", C), ("Wq", C), ("Wk", C), ("Wv", C), ("W1", 2 * C), ("W2", 2 * C),
           ("maa_w1", 2 * 160), ("maa_w2", E), ("decay_w1", 2 * ND),
           ("WrT", 2 * E), ("WkT", 2 * E), ("WvT", 2 * E), ("WgT", 2 * E), ("WoT", 2 * E),
           ("FkT", 2 * E), ("FrT", 2 * E), ("FvT", 2 * E), ("heads", 16), ("mean", 1), ("Wo", 2 * C),
           ("maa_w2_last", E), ("decay_w2", E)]
WCOL = {}
_at = 0
for _n, _w in WEIGHTS:
    WCOL[_n] = (_at, _w)
    _at += _w
NW = _at


def build(nc, x, ctx_in, weights, vecs, pos, vones, first, out):
    with ExitStack() as stack:
        def sb(name, shape, dt=F32):
            return stack.enter_context(nc.sbuf_tensor(name, shape, dt))

        def sem(name):
            return stack.enter_context(nc.semaphore(name))

        U = range(UNROLL)
        W = sb("W", [128, NW])
        vec = sb("vec", [128, NVEC])
        pe_tab = sb("pe_tab", [128, T])
        ident_bf = sb("ident_bf", [128, 128], BF16)

        stacks = nc.dram_tensor("stacks", (UNROLL, 2, H0, SCORE_ROWS, T), BF16, kind="Internal").ap()
        values = nc.dram_tensor("values", (UNROLL, 2, 128, NT), F32, kind="Internal").ap()

        def w(name, a=0, n=None):
            c, width = WCOL[name]
            return W[:, c + a:c + a + (n if n is not None else width - a)]

        def v(name):
            return vec[:, VEC[name]:VEC[name] + 1]

        def per(name, shape, dt=F32):
            return [sb(f"{name}{u}", shape, dt) for u in U]

        v_rep = per("v_rep", [128, 2, S1, NT])
        xin, zsum, dev, devsq = [[v_rep[u][:, a, 4 * b:4 * b + 4, :].rearrange("p (s q) t -> p s (q t)", s=2) for u in U]
                                 for a in range(2) for b in range(2)]
        var0 = per("var0", [128, 4])
        rstd0 = per("rstd0", [128, 4])
        nrm = devsq
        qn = per("qn", [128, T])
        kvn = per("kvn", [128, T])
        parts = per("parts", [128, 3, 2, T], BF16)
        left = zsum
        q_stack = per("q_stack", [128, H0 // 2, T], BF16)
        k_stack = per("k_stack", [128, H0 // 2, T], BF16)
        v_pad = per("v_pad", [128, 2, H0, 128])
        top = per("top", [128, 2, H0])
        guard = per("guard", [128, 2, 2, H0], BF16)
        guard_t = per("guard_t", [2 * H0, T], BF16)
        rden = per("rden", [64, 2, T])
        ctxn = per("ctxn", [64, 2, T])
        res = per("res", [128, T])
        fdev = per("fdev", [128, T])
        fdevsq = per("fdevsq", [128, T])
        fvar = per("fvar", [128, 2])
        frstd = per("frstd", [128, 2])
        fn1 = per("fn1", [128, T])
        fn = per("fn", [128, T])
        hid = per("hid", [128, 2, T])
        x1 = per("x1", [128, E])
        prev = per("prev", [128, 2, 2])
        s0 = per("s0", [128, 2, S1])
        stats = per("stats", [128, 2])
        mv = per("mv", [128, 1])
        rs1 = per("rs1", [128, 1])
        xh = per("xh", [128, E])
        xd = per("xd", [128, E])
        xt = per("xt", [128, 2, NT + 1])
        sx = per("sx", [128, 2, NT])
        xx = per("xx", [128, 2, NT])
        th = per("th", [128, 2, NT])
        mix = per("mix", [128, 5, 2, NT])
        mixed = mix
        rk = per("rk", [128, 2, 2, NT])
        vt = per("vt", [128, 2, NT])
        dec1 = per("dec1", [ND, NT])
        dec2 = per("dec2", [128, 2, NT])
        dec = per("dec", [128, 2, NT])
        kv = v_rep
        st = per("st", [128, 2, S1, NT])
        probs = [[st[u][:, j, 0:4, :].rearrange("p (a b) t -> p a (b t)", a=2) for j in range(2)] for u in U]
        rst = st
        ruk = per("ruk", [128, 2, NT])
        csum = per("csum", [128, H1])
        att = per("att", [128, E])
        att2 = per("att2", [128, E])
        attsq = per("attsq", [128, E])
        hsum = per("hsum", [128, H1])
        hvar = per("hvar", [128, H1])
        hrs = per("hrs", [128, H1])
        gate = per("gate", [128, 2, NT])
        gate2 = per("gate2", [128, 2, NT])
        ag = per("ag", [128, 2, NT])
        ag2 = per("ag2", [128, 2, NT])
        x2 = per("x2", [128, E])
        kk = per("kk", [128, 2, NT])
        kk2 = per("kk2", [128, 2, NT])
        rr = per("rr", [128, E])
        rr2 = per("rr2", [128, E])
        y = xd
        yo = per("yo", [128, E])
        mhalf = sb("mhalf", [128, H1])

        bank = [[stack.enter_context(nc.psum_tensor(f"bank{u}_{j}", [128, 512], F32)) for j in range(4)] for u in U]

        s_const = sem("s_const")
        s_setup = sem("s_setup")
        names = ("zsum centred devs var vareps rstd spread qkvn q_k v_done parts v_padded scored top "
                 "guard guard_T guard_c scoreT probs_ready pv ctxn wo res fcentred fdevs fvar fvareps frstd fspread "
                 "fn ffn1 gelu ffn2 x1 mv1 rstd1 xh1 xh1_T xx1 maa1 tanh1 maa2 mixed rkv rk_sb v_sb gd dec1 dec2 dec2_p dec "
                 "kv st rst_low rst_high ruk att hsum1 hvareps hrs attn attn_T gexp ag wo1 x2 mv2 rstd2 xh2 xh2_T xkr "
                 "ffk ffr rexp kk ffv done").split()
        S = {n: sem("s_" + n) for n in names}

        S.update({(n, u): sem(f"s_{n}{u}") for n in ("x_in", "prev_in", "stacked", "guard_in", "v_rep", "spilled", "v_out", "out_done") for u in U})

        def nth(i, u, per_batch=1, upto=None):
            n = per_batch if upto is None else upto
            return i * (UNROLL * per_batch) + u * per_batch + n

        def landed(i, dmas=1):
            return i * (16 * dmas) + 16 * dmas

        block = stack.enter_context(nc.Block())
        OUTER = B // UNROLL

        class Chain:

            def __init__(self, eng, name, i, each):
                self.eng, self.i, self.each, self.n = eng, i, each, 0
                self.sem = chain_sems[name]

            def link(self, ins):
                self.n += 1
                ins.then_inc(self.sem, 1)
                self.eng.wait_ge(self.sem, self.i * self.each + self.n)

            def end(self):
                assert self.n == self.each, (self.n, self.each)

        chain_sems = {n: sem("s_chain_" + n) for n in ("dve", "act", "pool")}

        @block.sync
        def _(sp):
            sp.dma_start(W[:, :], weights).then_inc(s_const, 16)
            sp.dma_start(vec[:, :], vecs).then_inc(s_const, 16)
            sp.dma_start(pe_tab[:, :], pos).then_inc(s_const, 16)
            for u in U:
                sp.dma_start(v_pad[u][:, :, :, :], vones).then_inc(s_const, 16)
            with sp.Fori(0, OUTER) as i:
                for u in U:
                    b = i * UNROLL + u
                    sp.wait_ge(S["done"], i * UNROLL + UNROLL)
                    xb = x[bass.ds(b, 1), :, :].rearrange("a c t -> (a c) t")
                    cb = ctx_in[bass.ds(b, 1), :, :].rearrange("a c t -> (a c) t")
                    sp.dma_start(xin[u][:, 0, :], xb).then_inc(S["x_in", u], 16)
                    sp.dma_start(xin[u][:, 1, :], cb).then_inc(S["x_in", u], 16)
                    sp.dma_start(prev[u][:, :, :].rearrange("p h r -> p (h r)"),
                                 first[bass.ds(b, 1), :, 0:4].rearrange("a p n -> (a p) n")).then_inc(S["prev_in", u], 16)
                    sp.dma_start(s0[u][:, :, :].rearrange("p h d -> p (h d)"),
                                 first[bass.ds(b, 1), :, 4:20].rearrange("a p n -> (a p) n")).then_inc(S["prev_in", u], 16)
                for u in U:
                    if u == 0:
                        sp.wait_ge(s_setup, 2 + UNROLL)
                    sp.wait_ge(S["parts"], nth(i, u))
                    for side, which in enumerate((Q_PARTS, K_PARTS)):
                        for r, part in enumerate(which):
                            sp.dma_start(stacks[u, side].rearrange("h (r d) t -> r h d t", d=D0)[r], parts[u][:, part, side, :]
                                         ).then_inc(S["spilled", u], 16)
                for u in U:
                    sp.wait_ge(S["spilled", u], landed(i, 12))
                    for side, dst in enumerate((q_stack, k_stack)):
                        for e in range(2):
                            sp.dma_start(dst[u][64 * e:64 * e + SCORE_ROWS, :, :],
                                         stacks[u, side].rearrange("(g e) r t -> e r g t", e=2)[e]).then_inc(S["stacked", u], 16)
                for u in U:
                    sp.wait_ge(S["guard_c"], nth(i, u))
                    for part in range(2):
                        for e in range(2):
                            row = 64 * e + SCORE_ROWS + part
                            sp.dma_start(q_stack[u][row:row + 1, :, :], guard_t[u][part * H0 + e:part * H0 + H0:2, :]
                                         ).then_inc(S["guard_in", u], 16)
                for u in U:
                    sp.wait_ge(S["v_sb"], nth(i, u))
                    sp.dma_start(values[u].rearrange("h p t -> p h t"), vt[u][:, :, :]).then_inc(S["v_out", u], 16)
                for u in U:
                    sp.wait_ge(S["v_out", u], landed(i))
                    for h in range(2):
                        sp.dma_start(v_rep[u][:, h, :, :], values[u, h].rearrange("(g d) t -> g (d t)", d=S1)[:, None, :]
                                     .broadcast_to([16, S1, S1 * NT])).then_inc(S["v_rep", u], 16)
                for u in U:
                    b = i * UNROLL + u
                    sp.wait_ge(S["done"], i * UNROLL + UNROLL + u + 1)
                    sp.dma_start(out[bass.ds(b, 1), :, :].rearrange("a l e -> (a l) e"), yo[u][:, :]).then_inc(S["out_done", u], 16)
            for u in U:
                sp.wait_ge(S["out_done", u], 16 * OUTER + 16)

        @block.tensor
        def _(pe):
            pe.wait_ge(s_const, 16 * (3 + UNROLL))
            pe.wait_ge(s_setup, 2 + UNROLL)
            ident = w("ident")
            with pe.Fori(0, OUTER) as i:
                def each(stage):
                    for u in U:
                        stage(u, bank[u])

                def centre(u, bk):
                    pe.wait_ge(S["zsum"], nth(i, u))
                    pe.matmul(bk[0][:, :], w("center"), zsum[u][:, :, :].rearrange("p a t -> p (a t)"), start=True, stop=True).then_inc(S["centred"], 1)
                each(centre)

                def variance(u, bk):
                    pe.wait_ge(S["devs"], nth(i, u, 2))
                    for j in range(4):
                        mm = pe.matmul(bk[1][:, j:j + 1], devsq[u][:, j // 2, (j % 2) * 128:(j % 2) * 128 + 128],
                                       w("mean"), start=True, stop=True)
                    mm.then_inc(S["var"], 1)
                each(variance)

                def spread(u, bk):
                    pe.wait_ge(S["rstd"], nth(i, u))
                    for j in range(4):
                        mm = pe.matmul(bk[2][:, j * 128:(j + 1) * 128], rstd0[u][:, j:j + 1].broadcast_to([128, 128]), ident,
                                       start=True, stop=True)
                    mm.then_inc(S["spread"], 1)
                each(spread)

                def project(u, bk):
                    pe.wait_ge(S["qkvn"], nth(i, u))
                    pe.matmul(bk[0][:, 0:T], w("Wq"), qn[u][:, :], start=True, stop=True)
                    pe.matmul(bk[0][:, T:2 * T], w("Wk"), kvn[u][:, :], start=True, stop=True).then_inc(S["q_k"], 1)
                    for j in range(2):
                        mm = pe.matmul(bk[1][:, j * 128:(j + 1) * 128], kvn[u][:, j * 128:(j + 1) * 128], w("Wv"),
                                       start=True, stop=True)
                    mm.then_inc(S["v_done"], 1)
                each(project)

                def scores(u, bk, h):
                    if h == 0:
                        pe.wait_ge(S["stacked", u], landed(i, 4))
                    if h >= 2:
                        pe.wait_ge(S["top"], nth(i, u, H0, h - 1))
                    e = 64 * (h % 2)
                    for j in range(2):
                        mm = pe.matmul(bk[2 + h % 2][:, j * T:(j + 1) * T],
                                       q_stack[u][e:e + SCORE_ROWS, h // 2, j * 128:(j + 1) * 128],
                                       k_stack[u][e:e + SCORE_ROWS, h // 2, :], start=True, stop=True)
                    mm.then_inc(S["scored"], 1)
                for u in U:
                    for h in range(H0):
                        scores(u, bank[u], h)

                def guard_turn(u, bk):
                    pe.wait_ge(S["guard"], nth(i, u))
                    for j in range(2):
                        mm = pe.matmul(bk[0][0:2 * H0, j * 128:(j + 1) * 128], guard[u][:, j, :, :].rearrange("p a h -> p (a h)"),
                                       ident_bf[:, :], start=True, stop=True)
                    mm.then_inc(S["guard_T"], 1)
                each(guard_turn)

                def scores_t(u, bk, h):
                    if h == 0:
                        pe.wait_ge(S["guard_in", u], landed(i, 4))
                        pe.wait_ge(S["top"], nth(i, u, H0))
                    if h >= 2:
                        pe.wait_ge(S["probs_ready"], nth(i, u, H0, h - 1))
                    e = 64 * (h % 2)
                    for j in range(2):
                        mm = pe.matmul(bk[2 + h % 2][:, j * T:(j + 1) * T],
                                       k_stack[u][e:e + GUARD_ROWS, h // 2, j * 128:(j + 1) * 128],
                                       q_stack[u][e:e + GUARD_ROWS, h // 2, :], start=True, stop=True)
                    mm.then_inc(S["scoreT"], 1)

                def weigh(u, bk, h):
                    if h == 0:
                        pe.wait_ge(S["v_padded"], nth(i, u))
                    pe.wait_ge(S["probs_ready"], nth(i, u, H0, h + 1))
                    half = h // 8
                    for j in range(2):
                        mm = pe.matmul(bk[1][:, half * T:(half + 1) * T], v_pad[u][:, j, h, :], probs[u][h % 2][:, j, :],
                                       start=(h % 8 == 0 and j == 0), stop=(h % 8 == 7 and j == 1))
                    mm.then_inc(S["pv"], 1)
                for u in U:
                    for h in range(H0 + 1):
                        if h < H0:
                            scores_t(u, bank[u], h)
                        if h > 0:
                            weigh(u, bank[u], h - 1)

                def wo(u, bk):
                    pe.wait_ge(S["ctxn"], nth(i, u))
                    for half in range(2):
                        mm = pe.matmul(bk[0][:, 0:T], w("Wo", half * C, C)[0:64, :], ctxn[u][:, half, :], start=half == 0, stop=half == 1)
                    mm.then_inc(S["wo"], 1)
                each(wo)

                def fcentre(u, bk):
                    pe.wait_ge(S["res"], nth(i, u))
                    pe.matmul(bk[2][:, 0:T], w("center"), res[u][:, :], start=True, stop=True).then_inc(S["fcentred"], 1)
                each(fcentre)

                def fvariance(u, bk):
                    pe.wait_ge(S["fdevs"], nth(i, u, 2))
                    for j in range(2):
                        mm = pe.matmul(bk[3][:, j:j + 1], fdevsq[u][:, j * 128:(j + 1) * 128], w("mean"), start=True, stop=True)
                    mm.then_inc(S["fvar"], 1)
                each(fvariance)

                def fspread(u, bk):
                    pe.wait_ge(S["frstd"], nth(i, u))
                    for j in range(2):
                        mm = pe.matmul(bk[2][:, j * 128:(j + 1) * 128], frstd[u][:, j:j + 1].broadcast_to([128, 128]), ident,
                                       start=True, stop=True)
                    mm.then_inc(S["fspread"], 1)
                each(fspread)

                def ffn1(u, bk):
                    pe.wait_ge(S["fn"], nth(i, u))
                    for m in range(2):
                        mm = pe.matmul(bk[0][:, m * T:(m + 1) * T], w("W1", m * 128, 128), fn[u][:, :], start=True, stop=True)
                    mm.then_inc(S["ffn1"], 1)
                each(ffn1)

                def ffn2(u, bk):
                    pe.wait_ge(S["gelu"], nth(i, u))
                    for m in range(2):
                        mm = pe.matmul(bk[1][:, 0:T], w("W2", m * 128, 128), hid[u][:, m, :], start=m == 0, stop=m == 1)
                    mm.then_inc(S["ffn2"], 1)
                each(ffn2)

                def turn1(u, bk):
                    pe.wait_ge(S["xh1"], nth(i, u))
                    for h in range(2):
                        mm = pe.transpose(bk[2][:, h * 128:(h + 1) * 128], xh[u][:, h * 128:(h + 1) * 128], ident)
                    mm.then_inc(S["xh1_T"], 1)
                each(turn1)

                def maa1(u, bk):
                    pe.wait_ge(S["xx1"], nth(i, u))
                    for m, n in ((0, 128), (1, 32)):
                        for h in range(2):
                            mm = pe.matmul(bk[3][0:n, m * 128:(m + 1) * 128], w("maa_w1", h * 160 + m * 128, n), xx[u][:, h, :],
                                           start=h == 0, stop=h == 1)
                    mm.then_inc(S["maa1"], 1)
                each(maa1)

                def maa2(u, bk):
                    pe.wait_ge(S["tanh1"], nth(i, u, 2))
                    for g in range(5):
                        for h in range(2):
                            p0 = 32 * g if g < 4 else 0
                            wt = w("maa_w2" if g < 4 else "maa_w2_last", h * 128, 128)[p0:p0 + 32, :]
                            col = (g // 4) * 256 + h * 128
                            mm = pe.matmul(bk[g % 4][:, col:col + 128], wt, th[u][p0:p0 + 32, g // 4, :], start=True, stop=True)
                    mm.then_inc(S["maa2"], 1)
                each(maa2)

                def channelwise(dst, name, src):
                    for m in range(2):
                        for h in range(2):
                            mm = pe.matmul(dst[:, m * 128:(m + 1) * 128], w(name, h * E + m * 128, 128), src[:, h, :],
                                           start=h == 0, stop=h == 1)
                    return mm

                def tokenwise(dst, name, src):
                    for h in range(2):
                        mm = pe.matmul(dst, src[:, h, :], w(name, h * E, E), start=h == 0, stop=h == 1)
                    return mm

                def rkv(u, bk):
                    pe.wait_ge(S["mixed"], nth(i, u))
                    channelwise(bk[0][:, 0:E], "WvT", mixed[u][:, MIX_V]).then_inc(S["rkv"], 1)
                    channelwise(bk[3][:, 0:E], "WrT", mixed[u][:, MIX_R])
                    channelwise(bk[3][:, E:2 * E], "WkT", mixed[u][:, MIX_K]).then_inc(S["rkv"], 1)
                    for h in range(2):
                        mm = pe.matmul(bk[2][0:ND, 0:NT], w("decay_w1", h * ND, ND), mixed[u][:, MIX_W, h, :], start=h == 0, stop=h == 1)
                    mm.then_inc(S["gd"], 1)
                    channelwise(bk[1][:, 0:E], "WgT", mixed[u][:, MIX_G]).then_inc(S["gd"], 1)
                each(rkv)

                def decay(u, bk):
                    pe.wait_ge(S["dec1"], nth(i, u))
                    for m in range(2):
                        mm = pe.matmul(bk[2][:, 256 + m * 128:256 + (m + 1) * 128], w("decay_w2", m * 128, 128)[0:ND, :], dec1[u][:, :],
                                       start=True, stop=True)
                    mm.then_inc(S["dec2_p"], 1)
                    pe.wait_ge(S["v_sb"], nth(i, u))
                    tokenwise(bk[0][:, 0:E], "WvT", mixed[u][:, MIX_V]).then_inc(S["dec2_p"], 1)
                each(decay)

                def attend(u, bk):
                    pe.wait_ge(S["ruk"], nth(i, u))
                    for h in range(2):
                        pe.matmul(bk[3][:, 256 + h * 16:256 + h * 16 + 16], ruk[u][:, h, :], w("heads"), start=True, stop=True)
                    pe.wait_ge(S["rst_low"], nth(i, u))
                    pe.wait_ge(S["rst_high"], nth(i, u))
                    for h in range(2):
                        for d in range(S1):
                            mm = pe.matmul(bk[3][:, (h * S1 + d) * 16:(h * S1 + d + 1) * 16], rst[u][:, h, d, :], w("heads"),
                                           start=True, stop=True)
                    mm.then_inc(S["att"], 1)
                each(attend)

                def turn_att(u, bk):
                    pe.wait_ge(S["attn"], nth(i, u))
                    for h in range(2):
                        mm = pe.transpose(bk[2][:, h * 128:(h + 1) * 128], att[u][:, h * 128:(h + 1) * 128], ident)
                    mm.then_inc(S["attn_T"], 1)
                each(turn_att)

                def wo1(u, bk):
                    pe.wait_ge(S["ag"], nth(i, u))
                    tokenwise(bk[0][:, 0:E], "WoT", ag2[u]).then_inc(S["wo1"], 1)
                each(wo1)

                def turn2(u, bk):
                    pe.wait_ge(S["xh2"], nth(i, u))
                    for h in range(2):
                        mm = pe.transpose(bk[2][:, h * 128:(h + 1) * 128], xh[u][:, h * 128:(h + 1) * 128], ident)
                    mm.then_inc(S["xh2_T"], 1)
                each(turn2)

                def ff_in(u, bk):
                    pe.wait_ge(S["xkr"], nth(i, u))
                    channelwise(bk[3][:, 0:E], "FkT", mixed[u][:, 0]).then_inc(S["ffk"], 1)
                    tokenwise(bk[0][:, 0:E], "FrT", mixed[u][:, 1]).then_inc(S["ffr"], 1)
                each(ff_in)

                def ff_out(u, bk):
                    pe.wait_ge(S["kk"], nth(i, u))
                    tokenwise(bk[1][:, 0:E], "FvT", kk2[u]).then_inc(S["ffv"], 1)
                each(ff_out)

        @block.scalar
        def _(act):
            act.wait_ge(s_const, 16 * (3 + UNROLL))
            with act.Fori(0, OUTER) as i:
                ch = Chain(act, "act", i, 5 * UNROLL)
                for u in U:
                    act.wait_ge(S["centred"], nth(i, u))
                    act.activation(dev[u][:, :, :], bank[u][0][:, :], ACT.Copy).then_inc(S["devs"], 1)
                    act.activation(devsq[u][:, :, :], bank[u][0][:, :], ACT.Square).then_inc(S["devs"], 1)
                for u in U:
                    act.wait_ge(S["v_done"], nth(i, u))
                    for j in range(2):
                        for s in range(2):
                            ins = act.activation(diag(v_pad[u], j, s), bank[u][1][:, j * 128 + s * 64:j * 128 + s * 64 + 64]
                                                 .rearrange("p (g d) -> p g d", d=D0), ACT.Copy)
                    ins.then_inc(S["v_padded"], 1)
                for u in U:
                    act.wait_ge(S["guard_T"], nth(i, u))
                    act.activation(guard_t[u][:, :], bank[u][0][0:2 * H0, 0:T], ACT.Copy).then_inc(S["guard_c"], 1)
                for u in U:
                    for h in range(H0):
                        act.wait_ge(S["scoreT"], nth(i, u, H0, h + 1))
                        if h >= 2:
                            act.wait_ge(S["pv"], nth(i, u, H0, h - 1))
                        act.activation(probs[u][h % 2][:, :, :], bank[u][2 + h % 2][:, :], ACT.Exp,
                                       scale=SCORE_SCALE).then_inc(S["probs_ready"], 1)
                for u in U:
                    act.wait_ge(S["fcentred"], nth(i, u))
                    act.activation(fdev[u][:, :], bank[u][2][:, 0:T], ACT.Copy).then_inc(S["fdevs"], 1)
                    act.activation(fdevsq[u][:, :], bank[u][2][:, 0:T], ACT.Square).then_inc(S["fdevs"], 1)
                for u in U:
                    act.wait_ge(S["ffn1"], nth(i, u))
                    for m in range(2):
                        ins = act.activation(hid[u][:, m, :], bank[u][0][:, m * T:(m + 1) * T], ACT.Gelu, bias=v(f"b1_{m}"))
                    ins.then_inc(S["gelu"], 1)
                for u in U:
                    act.wait_ge(S["maa1"], nth(i, u))
                    act.activation(th[u][:, 0, :], bank[u][3][:, 0:128], ACT.Tanh).then_inc(S["tanh1"], 1)
                    act.activation(th[u][0:32, 1, :], bank[u][3][0:32, 128:256], ACT.Tanh).then_inc(S["tanh1"], 1)
                for u in U:
                    act.wait_ge(S["rkv"], nth(i, u, 2, 1))
                    act.activation(vt[u][:, :, :], bank[u][0][:, 0:E], ACT.Copy).then_inc(S["v_sb"], 1)
                    act.wait_ge(S["rkv"], nth(i, u, 2))
                    act.activation(rk[u][:, :, :, :], bank[u][3][:, :], ACT.Copy).then_inc(S["rk_sb"], 1)
                    act.wait_ge(S["gd"], nth(i, u, 2, 1))
                    act.activation(dec1[u][:, :], bank[u][2][0:ND, 0:NT], ACT.Tanh).then_inc(S["dec1"], 1)
                for u in U:
                    act.wait_ge(S["dec2_p"], nth(i, u, 2, 1))
                    for m in range(2):
                        ch.link(act.activation(dec2[u][:, m, :], bank[u][2][:, 256 + m * 128:256 + (m + 1) * 128], ACT.Exp, bias=v(f"decay_{m}")))
                    act.activation(dec[u][:, :, :], dec2[u][:, :, :], ACT.Exp, scale=-1.0).then_inc(S["dec"], 1)
                    act.wait_ge(S["gd"], nth(i, u, 2))
                    ch.link(act.activation(gate2[u][:, :, :], bank[u][1][:, 0:E], ACT.Copy))
                    act.activation(gate[u][:, :, :], bank[u][1][:, 0:E], ACT.Exp, scale=-1.0).then_inc(S["gexp"], 1)
                for u in U:
                    act.wait_ge(S["ffk"], nth(i, u))
                    ch.link(act.activation(kk[u][:, :, :], bank[u][3][:, 0:E], ACT.Relu))
                    act.activation(kk2[u][:, :, :], kk[u][:, :, :], ACT.Square).then_inc(S["kk"], 1)
                    act.wait_ge(S["ffr"], nth(i, u))
                    ch.link(act.activation(rr[u][:, :], bank[u][0][:, 0:E], ACT.Exp, scale=-1.0))
                    act.activation(rr2[u][:, :], rr[u][:, :], ACT.Copy, bias=1.0).then_inc(S["rexp"], 1)
                ch.end()

        @block.gpsimd
        def _(pool):
            pool.memset(mhalf[:, :], -0.5).then_inc(s_setup, 1)
            for u in U:
                pool.memset(yo[u][:, 0:1], 0.0).then_inc(S["out_done", u], 16)
                pool.memset(x2[u][:, 0:1], 0.0).then_inc(S["done"], 1)
            for u in U:
                pool.memset(k_stack[u][:, :, :], 1.0).then_inc(s_setup, 1)
            pool.wait_ge(s_const, 16 * (3 + UNROLL))
            pool.tensor_copy(ident_bf[:, :], w("ident")).then_inc(s_setup, 1)
            pool.wait_ge(s_setup, 2 + UNROLL)
            with pool.Fori(0, OUTER) as i:
                for u in U:
                    pool.wait_ge(S["x_in", u], landed(i, 2))
                    pool.tensor_tensor(zsum[u][:, :, :], xin[u][:, :, :], pe_tab[:, None, :].broadcast_to([128, 2, T]), ALU.add).then_inc(S["zsum"], 1)
                for u in U:
                    pool.wait_ge(S["vareps"], nth(i, u))
                    pool.tensor_tensor(rstd0[u][:, :], var0[u][:, :], mhalf[:, 0:4], ALU.pow).then_inc(S["rstd"], 1)
                for u in U:
                    pool.wait_ge(S["fvareps"], nth(i, u))
                    pool.tensor_tensor(frstd[u][:, :], fvar[u][:, :], mhalf[:, 0:2], ALU.pow).then_inc(S["frstd"], 1)
                for u in U:
                    pool.wait_ge(S["mv1"], nth(i, u))
                    pool.tensor_tensor(rs1[u][:, :], mv[u][:, :], mhalf[:, 0:1], ALU.pow).then_inc(S["rstd1"], 1)
                for u in U:
                    pool.wait_ge(S["v_rep", u], landed(i, 2))
                    pool.wait_ge(S["rk_sb"], nth(i, u))
                    for h in range(2):
                        ins = pool.tensor_tensor(kv[u][:, h, :, :], v_rep[u][:, h, :, :], rk[u][:, 1, h, None, :].broadcast_to([128, S1, NT]), ALU.mult)
                    ins.then_inc(S["kv"], 1)
                for u in U:
                    pool.wait_ge(S["st"], nth(i, u, 2, 1))
                    pool.tensor_tensor(rst[u][:, 0, :, :], st[u][:, 0, :, :], rk[u][:, 0, 0, None, :].broadcast_to([128, S1, NT]), ALU.mult).then_inc(S["rst_low"], 1)
                for u in U:
                    pool.wait_ge(S["hvareps"], nth(i, u))
                    pool.tensor_tensor(hrs[u][:, :], hvar[u][:, :], mhalf[:, :], ALU.pow).then_inc(S["hrs"], 1)
                for u in U:
                    pool.wait_ge(S["mv2"], nth(i, u))
                    pool.tensor_tensor(rs1[u][:, :], mv[u][:, :], mhalf[:, 0:1], ALU.pow).then_inc(S["rstd2"], 1)

        @block.vector
        def _(dve):
            dve.wait_ge(s_const, 16 * (3 + UNROLL))
            with dve.Fori(0, OUTER) as i:
                ch = Chain(dve, "dve", i, DVE_LINKS * UNROLL)
                for u in U:
                    dve.wait_ge(S["var"], nth(i, u))
                    dve.tensor_scalar(var0[u][:, :], bank[u][1][:, 0:4], EPS, None, ALU.add).then_inc(S["vareps"], 1)
                for u in U:
                    dve.wait_ge(S["spread"], nth(i, u))
                    ch.link(dve.tensor_tensor(nrm[u][:, :, :], bank[u][2][:, :].rearrange("p (a t) -> p a t", a=2), dev[u][:, :, :], ALU.mult))
                    dve.tensor_scalar(qn[u][:, :], nrm[u][:, 0, :], v("ln_q_g"), v("ln_q_b"), ALU.mult, ALU.add)
                    dve.tensor_scalar(kvn[u][:, :], nrm[u][:, 1, :], v("ln_kv_g"), v("ln_kv_b"), ALU.mult, ALU.add).then_inc(S["qkvn"], 1)
                for u in U:
                    dve.wait_ge(S["q_k"], nth(i, u))
                    flat = lambda a: a.rearrange("p s t -> p (s t)")
                    ch.link(dve.tensor_copy(flat(parts[u][:, 0]), bank[u][0][:, :]))
                    ch.link(dve.tensor_tensor(flat(left[u][:, :, :]), bank[u][0][:, :], flat(parts[u][:, 0]), ALU.subtract))
                    ch.link(dve.tensor_copy(flat(parts[u][:, 1]), flat(left[u][:, :, :])))
                    dve.tensor_tensor(flat(parts[u][:, 2]), flat(left[u][:, :, :]), flat(parts[u][:, 1]), ALU.subtract).then_inc(S["parts"], 1)
                for u in U:
                    for h in range(H0):
                        dve.wait_ge(S["scored"], nth(i, u, H0, h + 1))
                        dve.tensor_reduce(top[u][:, :, h], bank[u][2 + h % 2][:, :].rearrange("p (a t) -> p a t", a=2), AX.X, ALU.max
                                          ).then_inc(S["top"], 1)
                    dve.wait_ge(S["top"], nth(i, u, H0))
                    ch.link(dve.tensor_scalar(guard[u][:, :, 0, :], top[u][:, :, :], -1.0, None, ALU.mult))
                    dve.scalar_tensor_tensor(out=guard[u][:, :, 1, :], in0=top[u][:, :, :], scalar=-1.0, in1=guard[u][:, :, 0, :],
                                             op0=ALU.mult, op1=ALU.subtract).then_inc(S["guard"], 1)
                for u in U:
                    dve.wait_ge(S["pv"], nth(i, u, H0))
                    flat = lambda a: a.rearrange("p s t -> p (s t)")
                    ch.link(dve.reciprocal(flat(rden[u][:, :, :]), bank[u][1][64:128, :]))
                    dve.tensor_tensor(flat(ctxn[u][:, :, :]), bank[u][1][0:64, :], flat(rden[u][:, :, :]), ALU.mult).then_inc(S["ctxn"], 1)
                for u in U:
                    dve.wait_ge(S["wo"], nth(i, u))
                    dve.tensor_tensor(res[u][:, :], bank[u][0][:, 0:T], qn[u][:, :], ALU.add).then_inc(S["res"], 1)
                for u in U:
                    dve.wait_ge(S["fvar"], nth(i, u))
                    dve.tensor_scalar(fvar[u][:, :], bank[u][3][:, 0:2], EPS, None, ALU.add).then_inc(S["fvareps"], 1)
                for u in U:
                    dve.wait_ge(S["fspread"], nth(i, u))
                    ch.link(dve.tensor_tensor(fn1[u][:, :], bank[u][2][:, 0:T], fdev[u][:, :], ALU.mult))
                    dve.tensor_scalar(fn[u][:, :], fn1[u][:, :], v("ffn_g"), v("ffn_b"), ALU.mult, ALU.add).then_inc(S["fn"], 1)

                def token_norm(u, src, mv_name):
                    ch.link(dve.tensor_reduce(stats[u][:, 0:1], src[u][:, :], AX.X, ALU.add))
                    ch.link(dve.scalar_tensor_tensor(out=xd[u][:, :], in0=stats[u][:, 0:1].broadcast_to([128, E]), scalar=-1.0 / E, in1=src[u][:, :],
                                                     op0=ALU.mult, op1=ALU.add))
                    ch.link(dve.tensor_tensor(att[u][:, :], xd[u][:, :], xd[u][:, :], ALU.mult))
                    ch.link(dve.tensor_reduce(stats[u][:, 1:2], att[u][:, :], AX.X, ALU.add))
                    dve.tensor_scalar(mv[u][:, :], stats[u][:, 1:2], 1.0 / E, EPS, ALU.mult, ALU.add).then_inc(S[mv_name], 1)

                def shift(u, g, b_, row):
                    src = bank[u][2]
                    dve.tensor_copy(xt[u][:, :, 0], prev[u][:, :, row])
                    for h in range(2):
                        ins = dve.tensor_scalar(xt[u][:, h, 1:NT + 1], src[:, h * 128:(h + 1) * 128], v(f"{g}_{h}"), v(f"{b_}_{h}"), ALU.mult, ALU.add)
                    ch.link(ins)
                    ch.link(dve.tensor_tensor(sx[u][:, :, :], xt[u][:, :, 0:NT], xt[u][:, :, 1:NT + 1], ALU.subtract))

                for u in U:
                    dve.wait_ge(S["ffn2"], nth(i, u))
                    ch.link(dve.scalar_tensor_tensor(out=x1[u][:, :], in0=bank[u][1][:, 0:T], scalar=v("b2"), in1=res[u][:, :],
                                                     op0=ALU.add, op1=ALU.add))
                    token_norm(u, x1, "mv1")
                for u in U:
                    dve.wait_ge(S["rstd1"], nth(i, u))
                    dve.tensor_scalar(xh[u][:, :], xd[u][:, :], rs1[u][:, :], None, ALU.mult).then_inc(S["xh1"], 1)
                for u in U:
                    dve.wait_ge(S["xh1_T"], nth(i, u))
                    dve.wait_ge(S["prev_in", u], landed(i, 2))
                    shift(u, "ln1_w", "ln1_b", 1)
                    for h in range(2):
                        ins = dve.scalar_tensor_tensor(out=xx[u][:, h, :], in0=sx[u][:, h, :], scalar=v(f"maa_x_{h}"), in1=xt[u][:, h, 1:NT + 1],
                                                       op0=ALU.mult, op1=ALU.add)
                    ins.then_inc(S["xx1"], 1)
                for u in U:
                    dve.wait_ge(S["maa2"], nth(i, u))
                    for g in range(5):
                        for h in range(2):
                            col = (g // 4) * 256 + h * 128
                            ins = dve.scalar_tensor_tensor(out=mix[u][:, g, h, :], in0=bank[u][g % 4][:, col:col + 128], scalar=v(f"stack{g}_{h}"),
                                                           in1=sx[u][:, h, :], op0=ALU.add, op1=ALU.mult)
                    ch.link(ins)
                    for h in range(2):
                        ins = dve.tensor_tensor(mixed[u][:, :, h, :], mix[u][:, :, h, :], xt[u][:, h, None, 1:NT + 1].broadcast_to([128, 5, NT]), ALU.add)
                    ins.then_inc(S["mixed"], 1)
                for u in U:
                    dve.wait_ge(S["rk_sb"], nth(i, u))
                    for h in range(2):
                        ins = dve.scalar_tensor_tensor(out=ruk[u][:, h, :], in0=rk[u][:, 0, h, :], scalar=v(f"faaaa_{h}"), in1=rk[u][:, 1, h, :],
                                                       op0=ALU.mult, op1=ALU.mult)
                    ins.then_inc(S["ruk"], 1)
                for u in U:
                    dve.wait_ge(S["kv"], nth(i, u))
                    dve.wait_ge(S["dec"], nth(i, u))
                    for h in range(2):
                        dve.tensor_copy(st[u][:, h, :, 0], s0[u][:, h, :])
                        for d in range(S1):
                            ins = dve.tensor_tensor_scan(st[u][:, h, d, 1:NT], dec[u][:, h, 0:NT - 1], kv[u][:, h, d, 0:NT - 1],
                                                         s0[u][:, h, d:d + 1], ALU.mult, ALU.add)
                        ins.then_inc(S["st"], 1)
                    dve.wait_ge(S["st"], nth(i, u, 2))
                    dve.tensor_tensor(rst[u][:, 1, :, :], st[u][:, 1, :, :], rk[u][:, 0, 1, None, :].broadcast_to([128, S1, NT]), ALU.mult).then_inc(S["rst_high"], 1)
                for u in U:
                    dve.wait_ge(S["att"], nth(i, u))
                    ch.link(dve.tensor_copy(csum[u][:, :], bank[u][3][:, 256:256 + H1]))
                    hd = lambda a: a[:, :].rearrange("p (h d) -> p h d", d=S1)
                    bc = lambda a: a[:, :, None].broadcast_to([128, H1, S1])
                    dve.wait_ge(S["dec2_p"], nth(i, u, 2))
                    ch.link(dve.tensor_tensor(hd(att2[u]), bank[u][0][:, 0:E].rearrange("p (h d) -> p h d", d=S1), bc(csum[u]), ALU.mult))
                    for h in range(2):
                        ins = dve.tensor_tensor(att[u][:, h * 128:(h + 1) * 128].rearrange("p (g d) -> p g d", d=S1),
                                                bank[u][3][:, h * 128:(h + 1) * 128].rearrange("p (d g) -> p g d", g=16),
                                                att2[u][:, h * 128:(h + 1) * 128].rearrange("p (g d) -> p g d", d=S1), ALU.add)
                    ch.link(ins)
                    ch.link(dve.tensor_reduce(hsum[u][:, :], hd(att[u]), AX.X, ALU.add))
                    ch.link(dve.scalar_tensor_tensor(out=hd(att2[u]), in0=bc(hsum[u]), scalar=-1.0 / S1, in1=hd(att[u]), op0=ALU.mult, op1=ALU.add))
                    ch.link(dve.tensor_tensor(attsq[u][:, :], att2[u][:, :], att2[u][:, :], ALU.mult))
                    ch.link(dve.tensor_reduce(hvar[u][:, :], hd(attsq[u]), AX.X, ALU.add))
                    dve.tensor_scalar(hvar[u][:, :], hvar[u][:, :], 1.0 / S1, EPS, ALU.mult, ALU.add).then_inc(S["hvareps"], 1)
                for u in U:
                    hd = lambda a: a[:, :].rearrange("p (h d) -> p h d", d=S1)
                    dve.wait_ge(S["hrs"], nth(i, u))
                    dve.tensor_tensor(hd(att[u]), hd(att2[u]), hrs[u][:, :, None].broadcast_to([128, H1, S1]), ALU.mult).then_inc(S["attn"], 1)
                for u in U:
                    dve.wait_ge(S["gexp"], nth(i, u))
                    ch.link(dve.tensor_scalar(gate[u][:, :, :], gate[u][:, :, :], 1.0, None, ALU.add))
                    ch.link(dve.reciprocal(gate[u][:, :, :], gate[u][:, :, :]))
                    ch.link(dve.tensor_tensor(gate2[u][:, :, :], gate2[u][:, :, :], gate[u][:, :, :], ALU.mult))
                    dve.wait_ge(S["attn_T"], nth(i, u))
                    for h in range(2):
                        ins = dve.tensor_scalar(ag[u][:, h, :], bank[u][2][:, h * 128:(h + 1) * 128], v(f"gn_w_{h}"), v(f"gn_b_{h}"), ALU.mult, ALU.add)
                    ch.link(ins)
                    dve.tensor_tensor(ag2[u][:, :, :], ag[u][:, :, :], gate2[u][:, :, :], ALU.mult).then_inc(S["ag"], 1)
                for u in U:
                    dve.wait_ge(S["wo1"], nth(i, u))
                    ch.link(dve.tensor_tensor(x2[u][:, :], bank[u][0][:, 0:E], x1[u][:, :], ALU.add))
                    token_norm(u, x2, "mv2")
                for u in U:
                    dve.wait_ge(S["rstd2"], nth(i, u))
                    dve.tensor_scalar(xh[u][:, :], xd[u][:, :], rs1[u][:, :], None, ALU.mult).then_inc(S["xh2"], 1)
                for u in U:
                    dve.wait_ge(S["xh2_T"], nth(i, u))
                    shift(u, "ln2_w", "ln2_b", 0)
                    for m, name in enumerate(("ffn_k", "ffn_r")):
                        for h in range(2):
                            ins = dve.scalar_tensor_tensor(out=mixed[u][:, m, h, :], in0=sx[u][:, h, :], scalar=v(f"{name}_{h}"),
                                                           in1=xt[u][:, h, 1:NT + 1], op0=ALU.mult, op1=ALU.add)
                    ins.then_inc(S["xkr"], 1)
                for u in U:
                    dve.wait_ge(S["rexp"], nth(i, u))
                    ch.link(dve.reciprocal(rr[u][:, :], rr2[u][:, :]))
                    dve.wait_ge(S["ffv"], nth(i, u))
                    ch.link(dve.tensor_tensor(y[u][:, :], bank[u][1][:, 0:E], rr[u][:, :], ALU.mult))
                    dve.wait_ge(S["out_done", u], i * 16 + 16)
                    dve.tensor_tensor(yo[u][:, :], y[u][:, :], x2[u][:, :], ALU.add).then_inc(S["done"], 1)
                ch.end()


DVE_LINKS = 35


def diag(v_pad, j, s):
    ap = v_pad[:, j, s * 8:(s + 1) * 8, 0:D0]
    dims = [list(d) for d in ap.ap]
    dims[1][0] += D0
    return bass.AP(tensor=ap.tensor, offset=ap.offset, ap=dims)


def kernel(**inputs):
    import concourse.bacc as bacc
    from concourse.bass_utils import run_bass_kernel_spmd as run

    f = {k: np.asarray(a) for k, a in inputs.items()}
    L0 = {k[len("L0_xattn_"):]: a for k, a in f.items() if k.startswith("L0_")}
    L1 = {k[len("L1_xattn_"):]: a for k, a in f.items() if k.startswith("L1_")}

    def tiles(a, k=128):
        n = a.shape[0] // k
        return np.ascontiguousarray(a.reshape(n, k, -1).transpose(1, 0, 2)).reshape(k, -1)

    W = np.zeros((128, NW), np.float32)

    def put(name, a):
        c, width = WCOL[name]
        assert a.shape[1] == width, (name, a.shape, width)
        W[:a.shape[0], c:c + width] = a

    eye = np.eye(128, dtype=np.float32)
    put("center", eye - np.float32(1.0 / C))
    put("ident", eye)
    put("mean", np.full((128, 1), 1.0 / C, np.float32))
    put("heads", (np.arange(128)[:, None] // S1 == np.arange(16)[None, :]).astype(np.float32))
    for n in ("Wq", "Wk", "Wv"):
        put(n, L0[n])
    put("W1", L0["W1"])
    put("W2", tiles(L0["W2"]))
    put("Wo", tiles(L0["Wo"], 64))
    put("maa_w1", tiles(L1["maa_w1"]))
    put("maa_w2", L1["maa_w2"][:4].reshape(128, E))
    put("maa_w2_last", L1["maa_w2"][4])
    put("decay_w1", tiles(L1["decay_w1"]))
    put("decay_w2", L1["decay_w2"])
    for n in ("Wr", "Wk", "Wv", "Wg", "Wo"):
        put(n + "T", tiles(L1[n].T))
    for n, m in (("Fk", "ffn_Wk"), ("Fr", "ffn_Wr"), ("Fv", "ffn_Wv")):
        put(n + "T", tiles(L1[m].T))

    V = np.zeros((128, NVEC), np.float32)
    cols = {"ln_q_g": L0["ln_q_g"], "ln_q_b": L0["ln_q_b"], "ln_kv_g": L0["ln_kv_g"], "ln_kv_b": L0["ln_kv_b"],
            "ffn_g": L0["ffn_ln_g"], "ffn_b": L0["ffn_ln_b"], "b1": L0["b1"], "b2": L0["b2"]}
    two = {"ln1_w": "ln1_w", "ln1_b": "ln1_b", "ln2_w": "ln2_w", "ln2_b": "ln2_b", "maa_x": "maa_x", "decay": "time_decay",
           "faaaa": "faaaa", "gn_w": "gn_w", "gn_b": "gn_b", "ffn_k": "ffn_maa_k", "ffn_r": "ffn_maa_r"}
    cols.update({n: L1[m].reshape(-1) for n, m in two.items()})
    cols.update({f"stack{g}": L1["maa_stack"][g] for g in range(5)})
    for n, a in cols.items():
        if a.size == 128:
            V[:, VEC[n]] = a
        else:
            for h in range(2):
                V[:, VEC[f"{n}_{h}"]] = a[h * 128:(h + 1) * 128]

    ang = np.arange(T, dtype=np.float32)[:, None] * np.exp(np.arange(0, C, 2, dtype=np.float32) * np.float32(-math.log(10000.0) / C))
    pos = np.zeros((T, C), np.float32)
    pos[:, 0::2], pos[:, 1::2] = np.sin(ang), np.cos(ang)
    pos = np.ascontiguousarray(pos.T)
    vones = np.zeros((128, 2, H0, 128), np.float32)
    for h in range(H0):
        vones[:, :, h, 64 + (h % 8) * 8:64 + (h % 8) * 8 + 8] = 1.0

    before = f["ctx_2048"][:, 0:2].reshape(B, 2, 2, 128).transpose(0, 3, 2, 1).reshape(B, 128, 4)
    state = f["ctx_2048"][:, 2:2 + S1].reshape(B, 2, 128, S1).transpose(0, 2, 1, 3).reshape(B, 128, 2 * S1)
    first = np.ascontiguousarray(np.concatenate([before, state], axis=2))

    nc = bacc.Bacc("TRN2", target_bir_lowering=False, num_devices=1)
    arrays = {"in_x": np.ascontiguousarray(f["x"]), "in_ctx": np.ascontiguousarray(f["ctx_2048"]), "in_weights": W, "in_vecs": V,
              "in_pos": pos, "in_vones": vones, "in_first": first}
    aps = [nc.dram_tensor(n, a.shape, mybir.dt.from_np(a.dtype), kind="ExternalInput").ap() for n, a in arrays.items()]
    out = nc.dram_tensor("out", (B, NT, E), F32, kind="ExternalOutput").ap()
    build(nc, *aps, out)
    r = run(nc, [arrays], core_ids=[0])
    return r.results[0]["out"]
```

```python
from contextlib import ExitStack
import math

import numpy as np
import concourse.bass as bass
from concourse import mybir

F32 = mybir.dt.float32
BF16 = mybir.dt.bfloat16
ALU = mybir.AluOpType
ACT = mybir.ActivationFunctionType
AX = mybir.AxisListType

B, C, T = 8, 128, 256
H0, D0 = 16, 8
NT = C
E = T
H1, S1 = 32, 8
NM = 32
ND = 64
EPS = 1e-5
SCORE_SCALE = 1.0 / math.sqrt(D0)
PRODUCTS = 6
Q_ROWS = (slice(0, 3), slice(3, 6, 2), slice(4, 5))
K_ROWS = (slice(2, 5), slice(0, 6, 5), slice(1, 2))
SCORE_ROWS = PRODUCTS * D0
GUARD_ROWS = SCORE_ROWS + 2
MIX_K, MIX_W, MIX_V, MIX_R, MIX_G = range(5)

VEC_NAMES = ["ln_q_g", "ln_q_b", "ln_kv_g", "ln_kv_b", "ffn_g", "ffn_b", "b1_0", "b1_1", "b2"]
VEC_NAMES += [f"{n}_{h}" for n in ("ln1_w", "ln1_b", "ln2_w", "ln2_b", "maa_x", "stack0", "stack1", "stack2", "stack3",
                                   "stack4", "decay", "faaaa", "gn_w", "gn_b", "ffn_k", "ffn_r") for h in range(2)]
VEC = {n: j for j, n in enumerate(VEC_NAMES)}
NVEC = len(VEC_NAMES)

WEIGHTS = [("center", C), ("ident", C), ("Wq", C), ("Wk", C), ("Wv", C), ("mean", 1), ("W1", 2 * C), ("W2", 2 * C),
           ("maa_w1", 2 * 160), ("maa_w2_0", E), ("maa_w2_1", E), ("maa_w2_2", E), ("maa_w2_3", E), ("maa_w2_4", E), ("decay_w1", 2 * ND),
           ("WrT", 2 * E), ("WkT", 2 * E), ("WvT", 2 * E), ("WgT", 2 * E), ("WoT", 2 * E),
           ("FkT", 2 * E), ("FrT", 2 * E), ("FvT", 2 * E), ("heads", 16), ("Wo", 2 * C),
           ("decay_w2", E)]
WCOL = {}
_at = 0
for _n, _w in WEIGHTS:
    WCOL[_n] = (_at, _w)
    _at += _w
NW = _at
NW_A = WCOL["W1"][0]


SLOTS = 130
A_CENTRE, A_VAR, A_SPREAD, A_AFFINE, A_PROJECT, A_PARTS = 49, 53, 58, 93, 95, 112
G_SCORES, G_STEP, G_GUARD = 15, 1, 33
G_SLOTS = [G_SCORES + n * G_STEP for n in range(H0)]
HEAD_FIRST, HEAD_STEP, HEAD_LAG = 4, 2, 2
HEAD_SLOTS = [HEAD_FIRST + n * HEAD_STEP for n in range(H0)]
H_CTX, H_WO, H_CENTRE, H_VAR, H_SPREAD, H_FFN1, H_FFN2 = 40, 51, 54, 54, 64, 64, 77
R_NORM, R_TURN, R_MAA1, R_MAA2, R_MIX, R_MAA3, R_MIX2, R_MIX3, R_MIXED = 1, 10, 20, 30, 30, 31, 32, 33, 33
R_RKV, R_DECAY, R_DECAY2, R_KV, R_SCAN, R_READ = 38, 47, 49, 56, 65, 78
R_SCAN_STEP = 2
R_SCAN_SLOTS = [R_SCAN + n * R_SCAN_STEP for n in range(4)]
O_ATTEND, O_HEADS, O_TURN_ATT, O_WO, O_TURN2, O_FF_IN, O_FF_OUT = 5, 8, 20, 34, 41, 52, 58


class Batch:

    def __init__(self, number, parity, of_parity):
        self.n, self.p, self.k = number, parity, of_parity


def turns(engine, turn):
    fixed = [Batch(n, n % 2, n // 2) for n in range(B)]

    def at(t):
        turn(*(fixed[t - lag] if 0 <= t - lag < B else None for lag in range(5)))

    for t in range(4):
        at(t)
    with engine.Fori(0, (B - 4) // 2) as j:
        even = [Batch(j * 2 + n, 0, j + n // 2) for n in (0, 2, 4)]
        odd = [Batch(j * 2 + n, 1, j + n // 2) for n in (1, 3, 5)]
        turn(even[2], odd[1], even[1], odd[0], even[0])
        turn(odd[2], even[2], odd[1], even[1], odd[0])
    for t in range(4 + (B - 4) // 2 * 2, B + 4):
        at(t)


def build(nc, x, ctx_in, weights, vecs, pos, first, out):
    with ExitStack() as stack:
        def sb(name, shape, dt=F32):
            return stack.enter_context(nc.sbuf_tensor(name, shape, dt))

        def two(name, shape, dt=F32):
            return [sb(f"{name}{p}", shape, dt) for p in range(2)]

        def psum(name):
            return stack.enter_context(nc.psum_tensor(name, [128, 512], F32))

        def sem(name):
            return stack.enter_context(nc.semaphore(name))

        def two_sems(name):
            return [sem(f"{name}{p}") for p in range(2)]

        W = sb("W", [128, NW])
        vec = sb("vec", [128, NVEC])
        pe_tab = sb("pe_tab", [128, T])
        ident_bf = sb("ident_bf", [128, 128], BF16)
        mhalf = sb("mhalf", [128, H1])

        def w(name, a=0, n=None):
            c, width = WCOL[name]
            return W[:, c + a:c + a + (n if n is not None else width - a)]

        def v(name):
            return vec[:, VEC[name]:VEC[name] + 1]

        xin = two("xin", [128, 2, T])
        zsum = sb("zsum", [128, 2, T])
        dev = sb("dev", [128, 2, T])
        devsq = sb("devsq", [128, 2, T])
        var_a = sb("var_a", [128, 4])
        rstd_a = sb("rstd_a", [128, 4])
        nrm = sb("nrm", [128, 2, T])
        qn = two("qn", [128, T])
        kvn = sb("kvn", [128, T])
        parts = sb("parts", [128, 3, 2, T], BF16)
        left = sb("left", [128, 2, T])
        q_stack = two("q_stack", [128, H0 // 2, T], BF16)
        k_stack = two("k_stack", [128, H0 // 2, T], BF16)
        v_pad = two("v_pad", [128, 2, H0, 128])
        top = sb("top", [128, 2, H0])
        guard = sb("guard", [128, 2, 2, H0], BF16)
        guard_t = sb("guard_t", [2 * H0, T], BF16)
        probs = [sb(f"probs{n}", [128, 2, T]) for n in range(PROBS)]
        rden = sb("rden", [64, 2 * T])
        ctxn = sb("ctxn", [64, 2 * T])
        res = sb("res", [128, T])
        dev_h = sb("dev_h", [128, T])
        devsq_h = sb("devsq_h", [128, T])
        var_h = sb("var_h", [128, 2])
        rstd_h = sb("rstd_h", [128, 2])
        nrm_h = sb("nrm_h", [128, T])
        fn = sb("fn", [128, T])
        hid = sb("hid", [128, 2, T])
        x1 = two("x1", [128, E])
        prev = two("prev", [128, 2, 2])
        s0 = two("s0", [128, 2, S1])
        stats = sb("stats", [128, 2])
        var_r = sb("var_r", [128, 1])
        rstd_r = sb("rstd_r", [128, 1])
        xd = sb("xd", [128, E])
        xdsq = sb("xdsq", [128, E])
        xh = sb("xh", [128, E])
        xt = sb("xt", [128, 2, NT + 1])
        sx = sb("sx", [128, 2, NT])
        xx = sb("xx", [128, 2, NT])
        th = sb("th", [128, 2, NT])
        mixed = sb("mixed", [128, 5, 2, NT])
        rk = sb("rk", [128, 2, 2, NT])
        vt = sb("vt", [128, 2, NT])
        v_rep = sb("v_rep", [128, 2, S1, NT])
        kv = v_rep
        dec1 = sb("dec1", [ND, NT])
        dec2 = sb("dec2", [128, 2, NT])
        dec = sb("dec", [128, 2, NT])
        st = sb("st", [128, 2, S1, NT])
        ruk = sb("ruk", [128, 2, NT])
        csum = sb("csum", [128, H1])
        att = sb("att", [128, E])
        att2 = sb("att2", [128, E])
        attsq = sb("attsq", [128, E])
        attn = sb("attn", [128, E])
        hsum = sb("hsum", [128, H1])
        hvar = sb("hvar", [128, H1])
        hrs = sb("hrs", [128, H1])
        gate_t = sb("gate_t", [128, 2, NT])
        gate_h = sb("gate_h", [128, 2, NT])
        gate = sb("gate", [128, 2, NT])
        ag = sb("ag", [128, 2, NT])
        agg = sb("agg", [128, 2, NT])
        vtok = sb("vtok", [128, E])
        stats_o = sb("stats_o", [128, 2])
        var_o = sb("var_o", [128, 1])
        rstd_o = sb("rstd_o", [128, 1])
        xd_o = sb("xd_o", [128, E])
        xdsq_o = sb("xdsq_o", [128, E])
        xh_o = sb("xh_o", [128, E])
        xt_o = sb("xt_o", [128, 2, NT + 1])
        sx_o = sb("sx_o", [128, 2, NT])
        x2 = sb("x2", [128, E])
        xkr = sb("xkr", [128, 2, 2, NT])
        kk = sb("kk", [128, 2, NT])
        kk2 = sb("kk2", [128, 2, NT])
        rr = sb("rr", [128, E])
        y = sb("y", [128, E])
        yo = two("yo", [128, E])

        stacks = nc.dram_tensor("stacks", (2, 2, C, PRODUCTS, T), BF16, kind="Internal").ap()
        values = nc.dram_tensor("values", (2, 2, 128, NT), F32, kind="Internal").ap()

        a_even, a_odd = psum("a_even"), psum("a_odd")
        h_even, h_odd, h_sum = psum("h_even"), psum("h_odd"), psum("h_sum")
        r_one, r_two = psum("r_one"), psum("r_two")
        o_bank = psum("o_bank")
        a_score, h_score = [a_even, a_odd], [h_even, h_odd]

        s_const, s_weights, s_setup, s_pads = (sem(n) for n in ("s_const", "s_weights", "s_setup", "s_pads"))
        s_x_in, s_prev_in, s_spilled, s_stacked, s_guard_in, s_v_out, s_v_rep, s_stored = (
            two_sems(n) for n in ("s_x_in", "s_prev_in", "s_spilled", "s_stacked", "s_guard_in", "s_v_out", "s_v_rep", "s_stored"))
        (s_zsum, s_centred, s_dev, s_var, s_vareps, s_rstd, s_spread, s_nrm, s_qkvn, s_qk, s_v, s_high, s_left, s_middle, s_parts,
         s_v_padded, s_scored, s_top, s_guard, s_guard_T, s_guard_c) = (sem("s_a_" + n) for n in (
             "zsum centred dev var vareps rstd spread nrm qkvn qk v high left middle parts "
             "v_padded scored top guard guard_T guard_c").split())
        (s_score_t, s_probs, s_sum, s_ctxn, s_wo, s_res, s_hcentred, s_hdev, s_hvar, s_hvareps, s_hrstd, s_hspread, s_hnrm, s_fn, s_ffn1,
         s_gelu, s_ffn2, s_x1) = (sem("s_h_" + n) for n in (
             "score_t probs sum ctxn wo res centred dev var vareps rstd spread nrm fn ffn1 gelu ffn2 x1").split())
        (s_var1, s_rstd1, s_xh1, s_xh1_T, s_xt1, s_xx1, s_maa1, s_tanh1, s_maa2, s_mix1, s_maa3, s_mixed, s_rk, s_vg, s_rk_sb, s_v_sb, s_gate, s_gated, s_dec1,
         s_dec1_sb, s_dec2, s_vtok, s_vtok_sb, s_dec, s_kv, s_st, s_rst_low, s_rst_high, s_ruk, s_att, s_hvareps1, s_hrs, s_attn, s_attn_T, s_ag, s_agg,
         s_wo1, s_var2, s_rstd2, s_xh2, s_xh2_T, s_xt2, s_xkr, s_ffkr, s_kk, s_sigm, s_ffv, s_done) = (sem("s_r_" + n) for n in (
             "var1 rstd1 xh1 xh1_T xt1 xx1 maa1 tanh1 maa2 mix1 maa3 mixed rk vg rk_sb v_sb gate gated dec1 dec1_sb dec2 vtok vtok_sb dec kv st rst_low rst_high "
             "ruk att hvareps hrs attn attn_T ag agg wo1 var2 rstd2 xh2 xh2_T xt2 xkr ffkr kk sigm ffv done").split())
        s_chain = {n: sem("s_chain_" + n) for n in ("dve_g", "dve_h", "dve_r", "dve_o", "act_r", "act_o")}

        class Chain:

            def __init__(self, eng, name, batch):
                self.eng, self.sem, self.each, self.batch, self.n = eng, s_chain[name], CHAINS[name], batch, 0

            def link(self, ins):
                self.n += 1
                ins.then_inc(self.sem, 1)
                self.eng.wait_ge(self.sem, self.batch.n * self.each + self.n)

            def end(self):
                assert self.n == self.each, (self.n, self.each)

        def dma(batch, count=1):
            return batch.k * (16 * count) + 16 * count

        flat = lambda ap: ap.rearrange("p a t -> p (a t)")
        block = stack.enter_context(nc.Block())

        @block.sync
        def _(sp):
            sp.dma_start(W[:, 0:NW_A], weights[:, 0:NW_A]).then_inc(s_const, 16)
            sp.dma_start(vec[:, :], vecs).then_inc(s_const, 16)
            sp.dma_start(pe_tab[:, :], pos).then_inc(s_const, 16)

            def turn(a, g, h, r, o):
                if a:
                    if not (isinstance(a.n, int) and a.n < 2):
                        sp.wait_ge(s_zsum, a.n - 1)
                    sp.dma_start(xin[a.p][:, 0, :], x[bass.ds(a.n, 1), :, :].rearrange("a c t -> (a c) t")).then_inc(s_x_in[a.p], 16)
                    sp.dma_start(xin[a.p][:, 1, :], ctx_in[bass.ds(a.n, 1), :, :].rearrange("a c t -> (a c) t")).then_inc(s_x_in[a.p], 16)
                if g:
                    sp.wait_ge(s_guard_c, g.n + 1)
                    for part in range(2):
                        for e in range(2):
                            row = 64 * e + SCORE_ROWS + part
                            sp.dma_start(q_stack[g.p][row:row + 1, :, :], guard_t[part * H0 + e:part * H0 + H0:2, :]
                                         ).then_inc(s_guard_in[g.p], 16)
                if r:
                    sp.wait_ge(s_v_sb, r.n + 1)
                    sp.dma_start(values[r.p].rearrange("h p t -> p h t"), vt[:, :, :]).then_inc(s_v_out[r.p], 16)
                    sp.wait_ge(s_v_out[r.p], dma(r))
                    for half in range(2):
                        sp.dma_start(v_rep[:, half, :, :], values[r.p, half].rearrange("(g d) t -> g (d t)", d=S1)[:, None, :]
                                     .broadcast_to([16, S1, S1 * NT])).then_inc(s_v_rep[r.p], 16)
                if o:
                    sp.wait_ge(s_done, o.n + 2)
                    sp.dma_start(out[bass.ds(o.n, 1), :, :].rearrange("a l e -> (a l) e"), yo[o.p][:, :]).then_inc(s_stored[o.p], 16)
                if h:
                    if not (isinstance(h.n, int) and h.n < 2):
                        sp.wait_ge(s_done, h.n)
                    sp.dma_start(flat(prev[h.p][:, :, :]), first[bass.ds(h.n, 1), :, 0:4].rearrange("a p n -> (a p) n")).then_inc(s_prev_in[h.p], 16)
                    sp.dma_start(flat(s0[h.p][:, :, :]), first[bass.ds(h.n, 1), :, 4:20].rearrange("a p n -> (a p) n")).then_inc(s_prev_in[h.p], 16)
                if a:
                    for part in range(3):
                        sp.wait_ge((s_high, s_middle, s_parts)[part], a.n + 1)
                        for side, which in enumerate((Q_ROWS, K_ROWS)):
                            rows = which[part]
                            sp.dma_start(stacks[a.p, side, :, rows, :], parts[:, part, side, None, :].broadcast_to([128, len(range(PRODUCTS)[rows]), T])
                                         ).then_inc(s_spilled[a.p], 16)
                    if isinstance(a.n, int) and a.n == 0:
                        sp.wait_ge(s_setup, SETUP)
                    sp.wait_ge(s_spilled[a.p], dma(a, 6))
                    for side, dst in enumerate((q_stack, k_stack)):
                        for e in range(2):
                            sp.dma_start(dst[a.p][64 * e:64 * e + SCORE_ROWS, :, :],
                                         stacks[a.p, side].rearrange("(i e d) r t -> e (d r) i t", e=2, d=D0)[e]).then_inc(s_stacked[a.p], 16)

            turns(sp, turn)
            for p in range(2):
                sp.wait_ge(s_stored[p], 16 * (B // 2 + 1))

        @block.tensor
        def _(pe):
            pe.wait_ge(s_const, CONSTS)
            pe.wait_ge(s_setup, SETUP)
            ident = w("ident")

            def channelwise(dst, name, src):
                for m in range(2):
                    for half in range(2):
                        mm = pe.matmul(dst[:, m * 128:(m + 1) * 128], w(name, half * E + m * 128, 128), src[:, half, :],
                                       start=half == 0, stop=half == 1)
                return mm

            def tokenwise(dst, name, src):
                for half in range(2):
                    mm = pe.matmul(dst, src[:, half, :], w(name, half * E, E), start=half == 0, stop=half == 1)
                return mm

            def token_mix(group, dst):
                for half in range(2):
                    mm = pe.matmul(dst[:, half * 128:(half + 1) * 128], w(f"maa_w2_{group}", half * 128, 128), th[:, group // 4, :],
                                   start=True, stop=True)
                return mm

            def turn(a, g, h, r, o):
                if h and isinstance(h.n, int) and h.n == 0:
                    pe.wait_ge(s_weights, 16)
                for slot in range(SLOTS):
                    if h and slot in HEAD_SLOTS:
                        head = HEAD_SLOTS.index(slot)
                        if head == 0:
                            pe.wait_ge(s_guard_in[h.p], dma(h, 4))
                            if not (isinstance(h.n, int) and h.n == 0):
                                pe.wait_ge(s_x1, h.n)
                        if head >= 2:
                            pe.wait_ge(s_probs, h.n * H0 + head - 1)
                        e = 64 * (head % 2)
                        for j in range(2):
                            mm = pe.matmul(h_score[head % 2][:, j * T:(j + 1) * T],
                                           k_stack[h.p][e:e + GUARD_ROWS, head // 2, j * 128:(j + 1) * 128],
                                           q_stack[h.p][e:e + GUARD_ROWS, head // 2, :], start=True, stop=True)
                        mm.then_inc(s_score_t, 1)
                    if g and slot in G_SLOTS:
                        head = G_SLOTS.index(slot)
                        if head == 0:
                            pe.wait_ge(s_stacked[g.p], dma(g, 4))
                            pe.wait_ge(s_v_padded, g.n + 1)
                        if head >= 2:
                            pe.wait_ge(s_top, g.n * H0 + head - 1)
                        e = 64 * (head % 2)
                        for j in range(2):
                            mm = pe.matmul(a_score[head % 2][:, j * T:(j + 1) * T],
                                           q_stack[g.p][e:e + SCORE_ROWS, head // 2, j * 128:(j + 1) * 128],
                                           k_stack[g.p][e:e + SCORE_ROWS, head // 2, :], start=True, stop=True)
                        mm.then_inc(s_scored, 1)
                    if g and slot == G_GUARD:
                        pe.wait_ge(s_guard, g.n + 1)
                        for j in range(2):
                            mm = pe.matmul(a_even[0:2 * H0, j * 128:(j + 1) * 128], guard[:, j, :, :].rearrange("p a h -> p (a h)"),
                                           ident_bf[:, :], start=True, stop=True)
                        mm.then_inc(s_guard_T, 1)
                    if a and slot == A_CENTRE:
                        pe.wait_ge(s_zsum, a.n + 1)
                        if not (isinstance(a.n, int) and a.n == 0):
                            pe.wait_ge(s_guard_c, a.n)
                        pe.matmul(a_even[:, :], w("center"), flat(zsum[:, :, :]), start=True, stop=True).then_inc(s_centred, 1)
                    if a and slot == A_VAR:
                        pe.wait_ge(s_dev, a.n * 2 + 2)
                        for j in range(4):
                            mm = pe.matmul(a_odd[:, j:j + 1], devsq[:, j // 2, (j % 2) * 128:(j % 2) * 128 + 128], w("mean"),
                                           start=True, stop=True)
                        mm.then_inc(s_var, 1)
                    if a and slot == A_SPREAD:
                        pe.wait_ge(s_rstd, a.n + 1)
                        for j in range(4):
                            mm = pe.matmul(a_odd[:, j * 128:(j + 1) * 128], rstd_a[:, j:j + 1].broadcast_to([128, 128]), ident,
                                           start=True, stop=True)
                        mm.then_inc(s_spread, 1)
                    if a and slot == A_PROJECT:
                        pe.wait_ge(s_qkvn, a.n * 2 + 2)
                        pe.matmul(a_even[:, 0:T], w("Wq"), qn[a.p][:, :], start=True, stop=True)
                        pe.matmul(a_even[:, T:2 * T], w("Wk"), kvn[:, :], start=True, stop=True).then_inc(s_qk, 1)
                        for j in range(2):
                            mm = pe.matmul(a_odd[:, j * 128:(j + 1) * 128], kvn[:, j * 128:(j + 1) * 128], w("Wv"), start=True, stop=True)
                        mm.then_inc(s_v, 1)
                    if r and slot == R_TURN:
                        pe.wait_ge(s_xh1, r.n + 1)
                        if not (isinstance(r.n, int) and r.n == 0):
                            pe.wait_ge(s_vtok_sb, r.n)
                        for half in range(2):
                            mm = pe.transpose(r_one[:, half * 128:(half + 1) * 128], xh[:, half * 128:(half + 1) * 128], ident)
                        mm.then_inc(s_xh1_T, 1)
                    if r and slot == R_MAA1:
                        pe.wait_ge(s_xx1, r.n + 1)
                        for m, n in ((0, 128), (1, 32)):
                            for half in range(2):
                                mm = pe.matmul(r_two[0:n, m * 128:(m + 1) * 128], w("maa_w1", half * 160 + m * 128, n), xx[:, half, :],
                                               start=half == 0, stop=half == 1)
                        mm.then_inc(s_maa1, 1)
                    if r and slot == R_MAA2:
                        pe.wait_ge(s_tanh1, r.n * 2 + 2)
                        for group in range(2):
                            mm = token_mix(group, r_one[:, group * 256:(group + 1) * 256])
                        mm.then_inc(s_maa2, 1)
                        for group in range(2):
                            mm = token_mix(2 + group, r_two[:, group * 256:(group + 1) * 256])
                        mm.then_inc(s_maa2, 1)
                    if r and slot == R_MAA3:
                        pe.wait_ge(s_mix1, r.n + 1)
                        token_mix(4, r_one[:, 0:256]).then_inc(s_maa3, 1)
                    if r and slot == R_RKV:
                        pe.wait_ge(s_mixed, r.n + 1)
                        channelwise(r_one[:, 0:E], "WvT", mixed[:, MIX_V])
                        channelwise(r_one[:, E:2 * E], "WgT", mixed[:, MIX_G]).then_inc(s_vg, 1)
                        channelwise(r_two[:, 0:E], "WrT", mixed[:, MIX_R])
                        channelwise(r_two[:, E:2 * E], "WkT", mixed[:, MIX_K]).then_inc(s_rk, 1)
                    if r and slot == R_DECAY:
                        pe.wait_ge(s_rk_sb, r.n + 1)
                        for half in range(2):
                            mm = pe.matmul(r_two[0:ND, 0:NT], w("decay_w1", half * ND, ND), mixed[:, MIX_W, half, :], start=half == 0, stop=half == 1)
                        mm.then_inc(s_dec1, 1)
                    if r and slot == R_DECAY2:
                        pe.wait_ge(s_dec1_sb, r.n + 1)
                        for m in range(2):
                            mm = pe.matmul(r_two[:, 128 + m * 128:128 + (m + 1) * 128], w("decay_w2", m * 128, 128)[0:ND, :], dec1[:, :],
                                           start=True, stop=True)
                        mm.then_inc(s_dec2, 1)
                        pe.wait_ge(s_gate, r.n * 2 + 2)
                        tokenwise(r_one[:, 0:E], "WvT", mixed[:, MIX_V]).then_inc(s_vtok, 1)
                    if o and slot == O_ATTEND:
                        pe.wait_ge(s_ruk, o.n + 1)
                        pe.wait_ge(s_done, o.n + 1)
                        for half in range(2):
                            pe.matmul(o_bank[:, E + half * 16:E + half * 16 + 16], ruk[:, half, :], w("heads"), start=True, stop=True)
                        for half in range(2):
                            if half == 0:
                                pe.wait_ge(s_rst_low, o.n + 1)
                            else:
                                pe.wait_ge(s_rst_high, o.n + 1)
                            for d in range(S1):
                                mm = pe.matmul(o_bank[:, (half * S1 + d) * 16:(half * S1 + d + 1) * 16], st[:, half, d, :], w("heads"),
                                               start=True, stop=True)
                        mm.then_inc(s_att, 1)
                    if o and slot == O_TURN_ATT:
                        pe.wait_ge(s_attn, o.n + 1)
                        for half in range(2):
                            mm = pe.transpose(o_bank[:, half * 128:(half + 1) * 128], attn[:, half * 128:(half + 1) * 128], ident)
                        mm.then_inc(s_attn_T, 1)
                    if o and slot == O_WO:
                        pe.wait_ge(s_agg, o.n + 1)
                        tokenwise(o_bank[:, 0:E], "WoT", agg).then_inc(s_wo1, 1)
                    if o and slot == O_TURN2:
                        pe.wait_ge(s_xh2, o.n + 1)
                        for half in range(2):
                            mm = pe.transpose(o_bank[:, half * 128:(half + 1) * 128], xh_o[:, half * 128:(half + 1) * 128], ident)
                        mm.then_inc(s_xh2_T, 1)
                    if o and slot == O_FF_IN:
                        pe.wait_ge(s_xkr, o.n + 1)
                        channelwise(o_bank[:, 0:E], "FkT", xkr[:, 0])
                        tokenwise(o_bank[:, E:2 * E], "FrT", xkr[:, 1]).then_inc(s_ffkr, 1)
                    if o and slot == O_FF_OUT:
                        pe.wait_ge(s_kk, o.n + 1)
                        pe.wait_ge(s_sigm, o.n + 1)
                        tokenwise(o_bank[:, 0:E], "FvT", kk2).then_inc(s_ffv, 1)

                    if h and slot - HEAD_LAG in HEAD_SLOTS:
                        head = HEAD_SLOTS.index(slot - HEAD_LAG)
                        pe.wait_ge(s_probs, h.n * H0 + head + 1)
                        for j in range(2):
                            mm = pe.matmul(h_sum[:, (head // 8) * T:(head // 8 + 1) * T], v_pad[h.p][:, j, head, :], probs[head % PROBS][:, j, :],
                                           start=(head % 8 == 0 and j == 0), stop=(head % 8 == 7 and j == 1))
                        mm.then_inc(s_sum, 1)
                    if h and slot == H_WO:
                        pe.wait_ge(s_ctxn, h.n + 1)
                        for half in range(2):
                            mm = pe.matmul(h_even[:, 0:T], w("Wo", half * C, C)[0:64, :], ctxn[:, half * T:(half + 1) * T], start=half == 0, stop=half == 1)
                        mm.then_inc(s_wo, 1)
                    if h and slot == H_CENTRE:
                        pe.wait_ge(s_res, h.n + 1)
                        pe.matmul(h_odd[:, 0:T], w("center"), res[:, :], start=True, stop=True).then_inc(s_hcentred, 1)
                    if h and slot == H_VAR:
                        pe.wait_ge(s_hdev, h.n * 2 + 2)
                        for j in range(2):
                            mm = pe.matmul(h_sum[:, j:j + 1], devsq_h[:, j * 128:(j + 1) * 128], w("mean"), start=True, stop=True)
                        mm.then_inc(s_hvar, 1)
                    if h and slot == H_SPREAD:
                        pe.wait_ge(s_hrstd, h.n + 1)
                        for j in range(2):
                            mm = pe.matmul(h_odd[:, j * 128:(j + 1) * 128], rstd_h[:, j:j + 1].broadcast_to([128, 128]), ident, start=True, stop=True)
                        mm.then_inc(s_hspread, 1)
                    if h and slot == H_FFN1:
                        pe.wait_ge(s_fn, h.n + 1)
                        for m in range(2):
                            mm = pe.matmul(h_even[:, m * T:(m + 1) * T], w("W1", m * 128, 128), fn[:, :], start=True, stop=True)
                        mm.then_inc(s_ffn1, 1)
                    if h and slot == H_FFN2:
                        pe.wait_ge(s_gelu, h.n + 1)
                        for m in range(2):
                            mm = pe.matmul(h_sum[:, 0:T], w("W2", m * 128, 128), hid[:, m, :], start=m == 0, stop=m == 1)
                        mm.then_inc(s_ffn2, 1)

            turns(pe, turn)

        @block.scalar
        def _(act):
            act.wait_ge(s_x_in[0], 32)
            act.dma_start(W[:, NW_A:NW], weights[:, NW_A:NW]).then_inc(s_weights, 16)
            act.wait_ge(s_const, CONSTS)
            act.wait_ge(s_pads, PADS)

            def turn(a, g, h, r, o):
                chain = Chain(act, "act_r", r) if r else None
                chain_o = Chain(act, "act_o", o) if o else None
                for slot in range(SLOTS):
                    if h and slot in HEAD_SLOTS:
                        head = HEAD_SLOTS.index(slot)
                        act.wait_ge(s_score_t, h.n * H0 + head + 1)
                        if head >= PROBS:
                            act.wait_ge(s_sum, h.n * H0 + head - PROBS + 1)
                        act.activation(flat(probs[head % PROBS][:, :, :]), h_score[head % 2][:, :], ACT.Exp, scale=SCORE_SCALE).then_inc(s_probs, 1)
                    if a and slot == A_CENTRE:
                        act.wait_ge(s_centred, a.n + 1)
                        act.activation(flat(devsq[:, :, :]), a_even[:, :], ACT.Square).then_inc(s_dev, 1)
                        act.activation(flat(dev[:, :, :]), a_even[:, :], ACT.Copy).then_inc(s_dev, 1)
                    if a and slot == A_AFFINE:
                        act.wait_ge(s_nrm, a.n + 1)
                        if not (isinstance(a.n, int) and a.n < 2):
                            act.wait_ge(s_res, a.n - 1)
                        act.activation(qn[a.p][:, :], nrm[:, 0, :], ACT.Identity, scale=v("ln_q_g"), bias=v("ln_q_b")).then_inc(s_qkvn, 1)
                        act.activation(kvn[:, :], nrm[:, 1, :], ACT.Identity, scale=v("ln_kv_g"), bias=v("ln_kv_b")).then_inc(s_qkvn, 1)
                    if a and slot == A_PARTS:
                        act.wait_ge(s_qk, a.n + 1)
                        act.activation(parts[:, 0].rearrange("p s t -> p (s t)"), a_even[:, :], ACT.Copy).then_inc(s_high, 1)
                        act.wait_ge(s_v, a.n + 1)
                        if not (isinstance(a.n, int) and a.n < 2):
                            act.wait_ge(s_sum, (a.n - 1) * H0)
                        for j in range(2):
                            for s in range(2):
                                ins = act.activation(diag(v_pad[a.p], j, s), a_odd[:, j * 128 + s * 64:j * 128 + s * 64 + 64]
                                                     .rearrange("p (g d) -> p g d", d=D0), ACT.Copy)
                        ins.then_inc(s_v_padded, 1)
                        act.wait_ge(s_left, a.n + 1)
                        act.activation(parts[:, 1].rearrange("p s t -> p (s t)"), flat(left[:, :, :]), ACT.Copy).then_inc(s_middle, 1)
                    if g and slot == G_GUARD:
                        act.wait_ge(s_guard_T, g.n + 1)
                        act.activation(guard_t[:, :], a_even[0:2 * H0, 0:T], ACT.Copy).then_inc(s_guard_c, 1)

                    if r and slot == R_TURN:
                        act.wait_ge(s_xh1_T, r.n + 1)
                        for half in range(2):
                            ins = act.activation(xt[:, half, 1:NT + 1], r_one[:, half * 128:(half + 1) * 128], ACT.Identity,
                                                 scale=v(f"ln1_w_{half}"), bias=v(f"ln1_b_{half}"))
                        ins.then_inc(s_xt1, 1)
                    if r and slot == R_MAA1:
                        act.wait_ge(s_maa1, r.n + 1)
                        act.activation(th[:, 0, :], r_two[:, 0:128], ACT.Tanh).then_inc(s_tanh1, 1)
                        act.activation(th[0:32, 1, :], r_two[0:32, 128:256], ACT.Tanh).then_inc(s_tanh1, 1)
                    if r and slot == R_RKV:
                        act.wait_ge(s_vg, r.n + 1)
                        act.activation(flat(vt[:, :, :]), r_one[:, 0:E], ACT.Copy).then_inc(s_v_sb, 1)
                        act.activation(flat(gate_t[:, :, :]), r_one[:, E:2 * E], ACT.Tanh, scale=0.5).then_inc(s_gate, 1)
                        act.activation(flat(gate_h[:, :, :]), r_one[:, E:2 * E], ACT.Copy, scale=0.5).then_inc(s_gate, 1)
                        act.wait_ge(s_rk, r.n + 1)
                        act.activation(rk[:, :, :, :].rearrange("p a b t -> p (a b t)"), r_two[:, :], ACT.Copy).then_inc(s_rk_sb, 1)
                    if r and slot == R_DECAY:
                        act.wait_ge(s_dec1, r.n + 1)
                        act.activation(dec1[:, :], r_two[0:ND, 0:NT], ACT.Tanh).then_inc(s_dec1_sb, 1)
                    if r and slot == R_DECAY2:
                        act.wait_ge(s_dec2, r.n + 1)
                        for m in range(2):
                            chain.link(act.activation(dec2[:, m, :], r_two[:, 128 + m * 128:128 + (m + 1) * 128], ACT.Exp, bias=v(f"decay_{m}")))
                        act.activation(flat(dec[:, :, :]), flat(dec2[:, :, :]), ACT.Exp, scale=-1.0).then_inc(s_dec, 1)
                        act.wait_ge(s_vtok, r.n + 1)
                        if not (isinstance(r.n, int) and r.n == 0):
                            act.wait_ge(s_hvareps1, r.n)
                        act.activation(vtok[:, :], r_one[:, 0:E], ACT.Copy).then_inc(s_vtok_sb, 1)
                    if o and slot == O_TURN_ATT:
                        act.wait_ge(s_attn_T, o.n + 1)
                        for half in range(2):
                            ins = act.activation(ag[:, half, :], o_bank[:, half * 128:(half + 1) * 128], ACT.Identity,
                                                 scale=v(f"gn_w_{half}"), bias=v(f"gn_b_{half}"))
                        ins.then_inc(s_ag, 1)
                    if o and slot == O_TURN2:
                        act.wait_ge(s_xh2_T, o.n + 1)
                        for half in range(2):
                            ins = act.activation(xt_o[:, half, 1:NT + 1], o_bank[:, half * 128:(half + 1) * 128], ACT.Identity,
                                                 scale=v(f"ln2_w_{half}"), bias=v(f"ln2_b_{half}"))
                        ins.then_inc(s_xt2, 1)
                    if o and slot == O_FF_IN:
                        act.wait_ge(s_ffkr, o.n + 1)
                        chain_o.link(act.activation(flat(kk[:, :, :]), o_bank[:, 0:E], ACT.Relu))
                        act.activation(flat(kk2[:, :, :]), flat(kk[:, :, :]), ACT.Square).then_inc(s_kk, 1)
                        act.activation(rr[:, :], o_bank[:, E:2 * E], ACT.Tanh, scale=0.5).then_inc(s_sigm, 1)

                    if h and slot == H_CENTRE:
                        act.wait_ge(s_hcentred, h.n + 1)
                        act.activation(devsq_h[:, :], h_odd[:, 0:T], ACT.Square).then_inc(s_hdev, 1)
                        act.activation(dev_h[:, :], h_odd[:, 0:T], ACT.Copy).then_inc(s_hdev, 1)
                    if h and slot == H_SPREAD:
                        act.wait_ge(s_hnrm, h.n + 1)
                        act.activation(fn[:, :], nrm_h[:, :], ACT.Identity, scale=v("ffn_g"), bias=v("ffn_b")).then_inc(s_fn, 1)
                    if h and slot == H_FFN1:
                        act.wait_ge(s_ffn1, h.n + 1)
                        for m in range(2):
                            ins = act.activation(hid[:, m, :], h_even[:, m * T:(m + 1) * T], ACT.Gelu, bias=v(f"b1_{m}"))
                        ins.then_inc(s_gelu, 1)
                for c in (chain, chain_o):
                    if c:
                        c.end()

            turns(act, turn)

        @block.gpsimd
        def _(pool):
            pool.memset(mhalf[:, :], -0.5).then_inc(s_setup, 1)
            pool.memset(th[:, :, :], 0.0).then_inc(s_setup, 1)
            for p in range(2):
                pool.memset(k_stack[p][:, :, :], 1.0).then_inc(s_setup, 1)
                pool.memset(yo[p][:, 0:1], 0.0).then_inc(s_stored[p], 16)
            pool.memset(x2[:, 0:1], 0.0).then_inc(s_done, 1)
            pool.wait_ge(s_const, CONSTS)
            pool.tensor_copy(ident_bf[:, :], w("ident")).then_inc(s_setup, 1)
            pool.wait_ge(s_setup, SETUP)

            def turn(a, g, h, r, o):
                for slot in range(SLOTS):
                    if a and slot == A_CENTRE:
                        pool.wait_ge(s_x_in[a.p], dma(a, 2))
                        if not (isinstance(a.n, int) and a.n == 0):
                            pool.wait_ge(s_spilled[1 - a.p], (a.k + (a.p - 1)) * 96 + 96)
                            pool.wait_ge(s_v_padded, a.n)
                        pool.tensor_tensor(zsum[:, :, :], xin[a.p][:, :, :], pe_tab[:, None, :].broadcast_to([128, 2, T]), ALU.add).then_inc(s_zsum, 1)
                    if a and slot == A_VAR:
                        pool.wait_ge(s_vareps, a.n + 1)
                        pool.tensor_tensor(rstd_a[:, :], var_a[:, :], mhalf[:, 0:4], ALU.pow).then_inc(s_rstd, 1)
                    if r and slot == R_NORM:
                        pool.wait_ge(s_var1, r.n + 1)
                        pool.tensor_tensor(rstd_r[:, :], var_r[:, :], mhalf[:, 0:1], ALU.pow).then_inc(s_rstd1, 1)
                    if r and slot == R_KV:
                        pool.wait_ge(s_v_rep[r.p], dma(r, 2))
                        pool.wait_ge(s_rk_sb, r.n + 1)
                        for half in range(2):
                            pool.tensor_tensor(kv[:, half, :, :], v_rep[:, half, :, :], rk[:, 1, half, None, :].broadcast_to([128, S1, NT]), ALU.mult
                                               ).then_inc(s_kv, 1)
                    if r and slot == R_READ:
                        pool.wait_ge(s_st, r.n * 2 + 1)
                        pool.tensor_tensor(st[:, 0, :, :], st[:, 0, :, :], rk[:, 0, 0, None, :].broadcast_to([128, S1, NT]), ALU.mult).then_inc(s_rst_low, 1)
                    if o and slot == O_HEADS:
                        pool.wait_ge(s_hvareps1, o.n + 1)
                        pool.tensor_tensor(hrs[:, :], hvar[:, :], mhalf[:, :], ALU.pow).then_inc(s_hrs, 1)
                    if o and slot == O_WO:
                        pool.wait_ge(s_var2, o.n + 1)
                        pool.tensor_tensor(rstd_o[:, :], var_o[:, :], mhalf[:, 0:1], ALU.pow).then_inc(s_rstd2, 1)
                    if h and slot == H_VAR:
                        pool.wait_ge(s_hvareps, h.n + 1)
                        pool.tensor_tensor(rstd_h[:, :], var_h[:, :], mhalf[:, 0:2], ALU.pow).then_inc(s_hrstd, 1)

            turns(pool, turn)

        @block.vector
        def _(dve):
            for p in range(2):
                dve.memset(v_pad[p][:, :, :, :], 0.0).then_inc(s_pads, 1)
            dve.wait_ge(s_pads, 2)
            for p in range(2):
                for j in range(2):
                    for half in range(2):
                        dve.memset(diag(v_pad[p], j, half, 64), 1.0).then_inc(s_pads, 1)
            dve.wait_ge(s_const, CONSTS)
            heads = lambda ap: ap.rearrange("p (h d) -> p h d", d=S1)
            every_d = lambda ap: ap[:, :, None].broadcast_to([128, H1, S1])

            def turn(a, g, h, r, o):
                chain_g = Chain(dve, "dve_g", g) if g else None
                chain_h = Chain(dve, "dve_h", h) if h else None
                chain_r = Chain(dve, "dve_r", r) if r else None
                chain_o = Chain(dve, "dve_o", o) if o else None

                def variance(chain, src, stats, xd, xdsq, var):
                    chain.link(dve.tensor_reduce(stats[:, 0:1], src[:, :], AX.X, ALU.add))
                    chain.link(dve.scalar_tensor_tensor(out=xd[:, :], in0=stats[:, 0:1].broadcast_to([128, E]), scalar=-1.0 / E, in1=src[:, :],
                                                          op0=ALU.mult, op1=ALU.add))
                    chain.link(dve.tensor_tensor(xdsq[:, :], xd[:, :], xd[:, :], ALU.mult))
                    chain.link(dve.tensor_reduce(stats[:, 1:2], xdsq[:, :], AX.X, ALU.add))
                    return dve.tensor_scalar(var[:, :], stats[:, 1:2], 1.0 / E, EPS, ALU.mult, ALU.add)

                def shifted(chain, xt, sx):
                    chain.link(dve.tensor_tensor(sx[:, :, :], xt[:, :, 0:NT], xt[:, :, 1:NT + 1], ALU.subtract))

                for slot in range(SLOTS):
                    if g and slot in G_SLOTS:
                        head = G_SLOTS.index(slot)
                        dve.wait_ge(s_scored, g.n * H0 + head + 1)
                        dve.tensor_reduce(top[:, :, head], a_score[head % 2][:, :].rearrange("p (a t) -> p a t", a=2), AX.X, ALU.max
                                          ).then_inc(s_top, 1)
                        if head == H0 - 1:
                            dve.wait_ge(s_top, g.n * H0 + H0)
                            chain_g.link(dve.tensor_scalar(guard[:, :, 0, :], top[:, :, :], -1.0, None, ALU.mult))
                            dve.scalar_tensor_tensor(out=guard[:, :, 1, :], in0=top[:, :, :], scalar=-1.0, in1=guard[:, :, 0, :],
                                                     op0=ALU.mult, op1=ALU.subtract).then_inc(s_guard, 1)
                    if a and slot == A_VAR:
                        dve.wait_ge(s_var, a.n + 1)
                        dve.tensor_scalar(var_a[:, :], a_odd[:, 0:4], EPS, None, ALU.add).then_inc(s_vareps, 1)
                    if a and slot == A_SPREAD:
                        dve.wait_ge(s_spread, a.n + 1)
                        dve.tensor_tensor(flat(nrm[:, :, :]), a_odd[:, :], flat(dev[:, :, :]), ALU.mult).then_inc(s_nrm, 1)
                    if a and slot == A_PARTS:
                        dve.wait_ge(s_high, a.n + 1)
                        dve.tensor_tensor(flat(left[:, :, :]), a_even[:, :], parts[:, 0].rearrange("p s t -> p (s t)"), ALU.subtract).then_inc(s_left, 1)
                        dve.wait_ge(s_middle, a.n + 1)
                        dve.tensor_tensor(parts[:, 2], left[:, :, :], parts[:, 1], ALU.subtract).then_inc(s_parts, 1)
                    if r and slot == R_NORM:
                        dve.wait_ge(s_x1, r.n + 1)
                        if not (isinstance(r.n, int) and r.n == 0):
                            dve.wait_ge(s_rst_low, r.n)
                            dve.wait_ge(s_rst_high, r.n)
                        variance(chain_r, x1[r.p], stats, xd, xdsq, var_r).then_inc(s_var1, 1)
                        dve.wait_ge(s_rstd1, r.n + 1)
                        dve.tensor_scalar(xh[:, :], xd[:, :], rstd_r[:, :], None, ALU.mult).then_inc(s_xh1, 1)
                        dve.wait_ge(s_prev_in[r.p], dma(r, 2))
                        chain_r.link(dve.tensor_copy(xt[:, :, 0], prev[r.p][:, :, 1]))
                    if r and slot == R_TURN:
                        dve.wait_ge(s_xt1, r.n + 1)
                        shifted(chain_r, xt, sx)
                        for half in range(2):
                            ins = dve.scalar_tensor_tensor(out=xx[:, half, :], in0=sx[:, half, :], scalar=v(f"maa_x_{half}"), in1=xt[:, half, 1:NT + 1],
                                                           op0=ALU.mult, op1=ALU.add)
                        ins.then_inc(s_xx1, 1)
                    for group in range(5):
                        if r and slot == (R_MIX, R_MIX, R_MIX2, R_MIX2, R_MIX3)[group]:
                            if group == 0:
                                dve.wait_ge(s_maa2, r.n * 2 + 1)
                            if group == 2:
                                dve.wait_ge(s_maa2, r.n * 2 + 2)
                            if group == 4:
                                dve.wait_ge(s_maa3, r.n + 1)
                            src = (r_one, r_one, r_two, r_two, r_one)[group]
                            for half in range(2):
                                col = (group % 2) * 256 + half * 128 if group < 4 else half * 128
                                ins = dve.scalar_tensor_tensor(out=mixed[:, group, half, :], in0=src[:, col:col + 128], scalar=v(f"stack{group}_{half}"),
                                                               in1=sx[:, half, :], op0=ALU.add, op1=ALU.mult)
                            if group == 1:
                                ins.then_inc(s_mix1, 1)
                            if group == 4:
                                chain_r.link(ins)
                    if r and slot == R_MIXED:
                        for half in range(2):
                            ins = dve.tensor_tensor(mixed[:, :, half, :], mixed[:, :, half, :], xt[:, half, None, 1:NT + 1].broadcast_to([128, 5, NT]), ALU.add)
                        ins.then_inc(s_mixed, 1)
                    if r and slot == R_DECAY2:
                        dve.wait_ge(s_rk_sb, r.n + 1)
                        if not (isinstance(r.n, int) and r.n == 0):
                            dve.wait_ge(s_att, r.n)
                            dve.wait_ge(s_agg, r.n)
                        for half in range(2):
                            ins = dve.scalar_tensor_tensor(out=ruk[:, half, :], in0=rk[:, 0, half, :], scalar=v(f"faaaa_{half}"), in1=rk[:, 1, half, :],
                                                           op0=ALU.mult, op1=ALU.mult)
                        ins.then_inc(s_ruk, 1)
                        dve.wait_ge(s_gate, r.n * 2 + 2)
                        dve.scalar_tensor_tensor(out=flat(gate[:, :, :]), in0=flat(gate_t[:, :, :]), scalar=1.0, in1=flat(gate_h[:, :, :]),
                                                 op0=ALU.add, op1=ALU.mult).then_inc(s_gated, 1)
                    if r and slot in R_SCAN_SLOTS:
                        half, quarter = divmod(R_SCAN_SLOTS.index(slot), 2)
                        if quarter == 0:
                            dve.wait_ge(s_kv, r.n * 2 + half + 1)
                            dve.wait_ge(s_dec, r.n + 1)
                            if not (isinstance(r.n, int) and r.n == 0):
                                dve.wait_ge(s_att, r.n)
                            dve.tensor_copy(st[:, half, :, 0], s0[r.p][:, half, :])
                        for d in range(quarter * S1 // 2, (quarter + 1) * S1 // 2):
                            ins = dve.tensor_tensor_scan(st[:, half, d, 1:NT], dec[:, half, 0:NT - 1], kv[:, half, d, 0:NT - 1],
                                                         s0[r.p][:, half, d:d + 1], ALU.mult, ALU.add)
                        if quarter == 1:
                            ins.then_inc(s_st, 1)
                    if r and slot == R_READ:
                        dve.wait_ge(s_st, r.n * 2 + 2)
                        dve.tensor_tensor(st[:, 1, :, :], st[:, 1, :, :], rk[:, 0, 1, None, :].broadcast_to([128, S1, NT]), ALU.mult).then_inc(s_rst_high, 1)
                    if o and slot == O_HEADS:
                        dve.wait_ge(s_att, o.n + 1)
                        dve.wait_ge(s_done, o.n + 1)
                        chain_o.link(dve.tensor_copy(csum[:, :], o_bank[:, E:E + H1]))
                        dve.wait_ge(s_vtok_sb, o.n + 1)
                        chain_o.link(dve.tensor_tensor(heads(att2[:, :]), heads(vtok[:, :]), every_d(csum), ALU.mult))
                        for half in range(2):
                            ins = dve.tensor_tensor(heads(att[:, half * 128:(half + 1) * 128]),
                                                    o_bank[:, half * 128:(half + 1) * 128].rearrange("p (d g) -> p g d", g=16),
                                                    heads(att2[:, half * 128:(half + 1) * 128]), ALU.add)
                        chain_o.link(ins)
                        chain_o.link(dve.tensor_reduce(hsum[:, :], heads(att[:, :]), AX.X, ALU.add))
                        chain_o.link(dve.scalar_tensor_tensor(out=heads(att2[:, :]), in0=every_d(hsum), scalar=-1.0 / S1, in1=heads(att[:, :]),
                                                              op0=ALU.mult, op1=ALU.add))
                        chain_o.link(dve.tensor_tensor(attsq[:, :], att2[:, :], att2[:, :], ALU.mult))
                        chain_o.link(dve.tensor_reduce(hvar[:, :], heads(attsq[:, :]), AX.X, ALU.add))
                        dve.tensor_scalar(hvar[:, :], hvar[:, :], 1.0 / S1, EPS, ALU.mult, ALU.add).then_inc(s_hvareps1, 1)
                    if o and slot == O_TURN_ATT:
                        dve.wait_ge(s_hrs, o.n + 1)
                        dve.tensor_tensor(heads(attn[:, :]), heads(att2[:, :]), every_d(hrs), ALU.mult).then_inc(s_attn, 1)
                        dve.wait_ge(s_ag, o.n + 1)
                        dve.wait_ge(s_gated, o.n + 1)
                        dve.tensor_tensor(agg[:, :, :], ag[:, :, :], gate[:, :, :], ALU.mult).then_inc(s_agg, 1)
                    if o and slot == O_WO:
                        dve.wait_ge(s_wo1, o.n + 1)
                        chain_o.link(dve.tensor_tensor(x2[:, :], o_bank[:, 0:E], x1[o.p][:, :], ALU.add))
                        variance(chain_o, x2, stats_o, xd_o, xdsq_o, var_o).then_inc(s_var2, 1)
                        chain_o.link(dve.tensor_copy(xt_o[:, :, 0], prev[o.p][:, :, 0]))
                        dve.wait_ge(s_rstd2, o.n + 1)
                        dve.tensor_scalar(xh_o[:, :], xd_o[:, :], rstd_o[:, :], None, ALU.mult).then_inc(s_xh2, 1)
                    if o and slot == O_TURN2:
                        dve.wait_ge(s_xt2, o.n + 1)
                        shifted(chain_o, xt_o, sx_o)
                        for m, name in enumerate(("ffn_k", "ffn_r")):
                            for half in range(2):
                                ins = dve.scalar_tensor_tensor(out=xkr[:, m, half, :], in0=sx_o[:, half, :], scalar=v(f"{name}_{half}"),
                                                               in1=xt_o[:, half, 1:NT + 1], op0=ALU.mult, op1=ALU.add)
                        ins.then_inc(s_xkr, 1)
                    if o and slot == O_FF_OUT:
                        dve.wait_ge(s_ffv, o.n + 1)
                        dve.wait_ge(s_sigm, o.n + 1)
                        chain_o.link(dve.scalar_tensor_tensor(out=y[:, :], in0=rr[:, :], scalar=1.0, in1=o_bank[:, 0:E], op0=ALU.add, op1=ALU.mult))
                        dve.wait_ge(s_stored[o.p], dma(o))
                        dve.scalar_tensor_tensor(out=yo[o.p][:, :], in0=y[:, :], scalar=0.5, in1=x2[:, :], op0=ALU.mult, op1=ALU.add).then_inc(s_done, 1)

                    if h and slot == H_CTX:
                        dve.wait_ge(s_sum, h.n * H0 + H0)
                        chain_h.link(dve.reciprocal(rden[:, :], h_sum[64:128, :]))
                        dve.tensor_tensor(ctxn[:, :], h_sum[0:64, :], rden[:, :], ALU.mult).then_inc(s_ctxn, 1)
                    if h and slot == H_WO:
                        dve.wait_ge(s_wo, h.n + 1)
                        dve.tensor_tensor(res[:, :], h_even[:, 0:T], qn[h.p][:, :], ALU.add).then_inc(s_res, 1)
                    if h and slot == H_VAR:
                        dve.wait_ge(s_hvar, h.n + 1)
                        dve.tensor_scalar(var_h[:, :], h_sum[:, 0:2], EPS, None, ALU.add).then_inc(s_hvareps, 1)
                    if h and slot == H_SPREAD:
                        dve.wait_ge(s_hspread, h.n + 1)
                        dve.tensor_tensor(nrm_h[:, :], h_odd[:, 0:T], dev_h[:, :], ALU.mult).then_inc(s_hnrm, 1)
                    if h and slot == H_FFN2:
                        dve.wait_ge(s_ffn2, h.n + 1)
                        if not (isinstance(h.n, int) and h.n < 2):
                            dve.wait_ge(s_done, h.n)
                        dve.scalar_tensor_tensor(out=x1[h.p][:, :], in0=h_sum[:, 0:T], scalar=v("b2"), in1=res[:, :], op0=ALU.add, op1=ALU.add
                                                 ).then_inc(s_x1, 1)
                for chain in (chain_g, chain_h, chain_r, chain_o):
                    if chain:
                        chain.end()

            turns(dve, turn)


PROBS = 3
SETUP = 5
CONSTS = 16 * 3
PADS = 2 + 8
CHAINS = {"dve_g": 1, "dve_h": 1, "dve_r": 7, "dve_o": 15, "act_r": 2, "act_o": 1}


def diag(v_pad, j, s, at=0):
    ap = v_pad[:, j, s * 8:(s + 1) * 8, at:at + D0]
    dims = [list(d) for d in ap.ap]
    dims[1][0] += D0
    return bass.AP(tensor=ap.tensor, offset=ap.offset, ap=dims)


def kernel(**inputs):
    import concourse.bacc as bacc
    from concourse.bass_utils import run_bass_kernel_spmd as run

    f = {k: np.asarray(a) for k, a in inputs.items()}
    L0 = {k[len("L0_xattn_"):]: a for k, a in f.items() if k.startswith("L0_")}
    L1 = {k[len("L1_xattn_"):]: a for k, a in f.items() if k.startswith("L1_")}

    def tiles(a, k=128):
        n = a.shape[0] // k
        return np.ascontiguousarray(a.reshape(n, k, -1).transpose(1, 0, 2)).reshape(k, -1)

    W = np.zeros((128, NW), np.float32)

    def put(name, a):
        c, width = WCOL[name]
        assert a.shape[1] == width, (name, a.shape, width)
        W[:a.shape[0], c:c + width] = a

    eye = np.eye(128, dtype=np.float32)
    put("center", eye - np.float32(1.0 / C))
    put("ident", eye)
    put("mean", np.full((128, 1), 1.0 / C, np.float32))
    put("heads", (np.arange(128)[:, None] // S1 == np.arange(16)[None, :]).astype(np.float32))
    for n in ("Wq", "Wk", "Wv"):
        put(n, L0[n])
    put("W1", L0["W1"])
    put("W2", tiles(L0["W2"]))
    put("Wo", tiles(L0["Wo"], 64))
    put("maa_w1", tiles(L1["maa_w1"]))
    for g in range(5):
        a = np.zeros((128, E), np.float32)
        a[32 * (g % 4):32 * (g % 4) + 32] = L1["maa_w2"][g]
        put(f"maa_w2_{g}", a)
    put("decay_w1", tiles(L1["decay_w1"]))
    put("decay_w2", L1["decay_w2"])
    for n in ("Wr", "Wk", "Wv", "Wg", "Wo"):
        put(n + "T", tiles(L1[n].T))
    for n, m in (("Fk", "ffn_Wk"), ("Fr", "ffn_Wr"), ("Fv", "ffn_Wv")):
        put(n + "T", tiles(L1[m].T))

    V = np.zeros((128, NVEC), np.float32)
    cols = {"ln_q_g": L0["ln_q_g"], "ln_q_b": L0["ln_q_b"], "ln_kv_g": L0["ln_kv_g"], "ln_kv_b": L0["ln_kv_b"],
            "ffn_g": L0["ffn_ln_g"], "ffn_b": L0["ffn_ln_b"], "b1": L0["b1"], "b2": L0["b2"]}
    two = {"ln1_w": "ln1_w", "ln1_b": "ln1_b", "ln2_w": "ln2_w", "ln2_b": "ln2_b", "maa_x": "maa_x", "decay": "time_decay",
           "faaaa": "faaaa", "gn_w": "gn_w", "gn_b": "gn_b", "ffn_k": "ffn_maa_k", "ffn_r": "ffn_maa_r"}
    cols.update({n: L1[m].reshape(-1) for n, m in two.items()})
    cols.update({f"stack{g}": L1["maa_stack"][g] for g in range(5)})
    for n, a in cols.items():
        if a.size == 128:
            V[:, VEC[n]] = a
        else:
            for h in range(2):
                V[:, VEC[f"{n}_{h}"]] = a[h * 128:(h + 1) * 128]

    ang = np.arange(T, dtype=np.float32)[:, None] * np.exp(np.arange(0, C, 2, dtype=np.float32) * np.float32(-math.log(10000.0) / C))
    pos = np.zeros((T, C), np.float32)
    pos[:, 0::2], pos[:, 1::2] = np.sin(ang), np.cos(ang)
    pos = np.ascontiguousarray(pos.T)

    before = f["ctx_2048"][:, 0:2].reshape(B, 2, 2, 128).transpose(0, 3, 2, 1).reshape(B, 128, 4)
    state = f["ctx_2048"][:, 2:2 + S1].reshape(B, 2, 128, S1).transpose(0, 2, 1, 3).reshape(B, 128, 2 * S1)
    first = np.ascontiguousarray(np.concatenate([before, state], axis=2))

    nc = bacc.Bacc("TRN2", target_bir_lowering=False, num_devices=1)
    arrays = {"in_x": np.ascontiguousarray(f["x"]), "in_ctx": np.ascontiguousarray(f["ctx_2048"]), "in_weights": W, "in_vecs": V,
              "in_pos": pos, "in_first": first}
    aps = [nc.dram_tensor(n, a.shape, mybir.dt.from_np(a.dtype), kind="ExternalInput").ap() for n, a in arrays.items()]
    out = nc.dram_tensor("out", (B, NT, E), F32, kind="ExternalOutput").ap()
    build(nc, *aps, out)
    r = run(nc, [arrays], core_ids=[0])
    return r.results[0]["out"]
```

```python
from contextlib import ExitStack
import math

import numpy as np
import concourse.bass as bass
from concourse import mybir

F32 = mybir.dt.float32
BF16 = mybir.dt.bfloat16
ALU = mybir.AluOpType
ACT = mybir.ActivationFunctionType
AX = mybir.AxisListType

B, C, T = 8, 128, 256
H0, D0 = 16, 8
NT = C
E = T
H1, S1 = 32, 8
ND = 64
EPS = 1e-5
SCORE_SCALE = 1.0 / math.sqrt(D0)
PRODUCTS = 6
Q_ROWS = (slice(0, 3), slice(3, 6, 2), slice(4, 5))
K_ROWS = (slice(2, 5), slice(0, 6, 5), slice(1, 2))
SCORE_ROWS = PRODUCTS * D0
GUARD_ROWS = SCORE_ROWS + 2
MIX_K, MIX_W, MIX_V, MIX_R, MIX_G = range(5)

VEC_NAMES = ["ln_q_g", "ln_q_b", "ln_kv_g", "ln_kv_b", "ffn_g", "ffn_b", "b1_0", "b1_1", "b2"]
VEC_NAMES += [f"{n}_{h}" for n in ("ln1_w", "ln1_b", "ln2_w", "ln2_b", "maa_x", "stack0", "stack1", "stack2", "stack3",
                                   "stack4", "decay", "faaaa", "gn_w", "gn_b", "ffn_k", "ffn_r") for h in range(2)]
VEC = {n: j for j, n in enumerate(VEC_NAMES)}
NVEC = len(VEC_NAMES)

WEIGHTS = [("center", C), ("ident", C), ("Wq", C), ("Wk", C), ("Wv", C), ("mean", 1), ("W1", 2 * C), ("W2", 2 * C),
           ("maa_w1", 2 * 160), ("maa_w2_0", E), ("maa_w2_1", E), ("maa_w2_2", E), ("maa_w2_3", E), ("maa_w2_4", E), ("decay_w1", 2 * ND),
           ("WrT", 2 * E), ("WkT", 2 * E), ("WvT", 2 * E), ("WgT", 2 * E), ("WoT", 2 * E),
           ("FkT", 2 * E), ("FrT", 2 * E), ("FvT", 2 * E), ("heads", 16), ("Wo", 2 * C),
           ("decay_w2", E)]
WCOL = {}
_at = 0
for _n, _w in WEIGHTS:
    WCOL[_n] = (_at, _w)
    _at += _w
NW = _at
NW_A = WCOL["W1"][0]


SLOTS = 73
A_CENTRE, A_VAR, A_SPREAD, A_AFFINE, A_PROJECT, A_PARTS = 52, 59, 65, 69, 72, 72
G_SLOTS = 19, 20, 21, 23, 24, 25, 28, 29, 30, 34, 35, 36, 37, 39, 42, 43
G_GUARD = 45
HEAD_SLOTS = 1, 2, 7, 9, 13, 16, 17, 19, 22, 27, 30, 31, 32, 40, 41, 43
HEAD_SUM_SLOTS = 2, 5, 12, 14, 17, 20, 22, 24, 26, 30, 35, 36, 37, 42, 43, 44
H_CTX_LOW, H_CTX, H_WO, H_CENTRE, H_VAR, H_SPREAD, H_FFN1, H_FFN2 = 51, 53, 55, 58, 59, 64, 68, 71
TO_GELU, TO_EXP = 63, 70
R_NORM, R_AGGR, R_EPS, R_XH, R_TURN, R_MAA1, R_MAA2, R_MIX, R_MAA3, R_MIX2, R_MIX3, R_MIXED = 3, 4, 4, 4, 12, 18, 29, 29, 32, 33, 36, 38
R_VG, R_RK, R_DECAY, R_DECAY2, R_OWN, R_KV, R_READ = 47, 49, 57, 60, 61, 66, 72
R_SCAN_SLOTS = 67, 68, 69, 70
O_TURN_ATT, O_AG, O_WO, O_NORM, O_AGGR, O_EPS, O_XH, O_TURN2, O_FF_IN, O_FF_OUT = 32, 37, 41, 46, 48, 50, 54, 56, 62, 68
O_ATTEND_SLOTS = 0, 1, 6, 8
O_HEADS_SLOTS = 8, 9, 10, 11, 14, 15


class Batch:

    def __init__(self, number, parity, of_parity):
        self.n, self.p, self.k = number, parity, of_parity


def turns(engine, turn):
    fixed = [Batch(n, n % 2, n // 2) for n in range(B)]

    def at(t):
        turn(*(fixed[t - lag] if 0 <= t - lag < B else None for lag in range(5)))

    for t in range(4):
        at(t)
    with engine.Fori(0, (B - 4) // 2) as j:
        even = [Batch(j * 2 + n, 0, j + n // 2) for n in (0, 2, 4)]
        odd = [Batch(j * 2 + n, 1, j + n // 2) for n in (1, 3, 5)]
        turn(even[2], odd[1], even[1], odd[0], even[0])
        turn(odd[2], even[2], odd[1], even[1], odd[0])
    for t in range(4 + (B - 4) // 2 * 2, B + 4):
        at(t)


def build(nc, x, ctx_in, weights, vecs, pos, first, out):
    with ExitStack() as stack:
        def sb(name, shape, dt=F32):
            return stack.enter_context(nc.sbuf_tensor(name, shape, dt))

        def two(name, shape, dt=F32):
            return [sb(f"{name}{p}", shape, dt) for p in range(2)]

        def psum(name):
            return stack.enter_context(nc.psum_tensor(name, [128, 512], F32))

        def sem(name):
            return stack.enter_context(nc.semaphore(name))

        def two_sems(name):
            return [sem(f"{name}{p}") for p in range(2)]

        W = sb("W", [128, NW])
        vec = sb("vec", [128, NVEC])
        pe_tab = sb("pe_tab", [128, T])
        ident_bf = sb("ident_bf", [128, 128], BF16)
        mhalf = sb("mhalf", [128, H1])
        table_out = sb("table_out", [128, 1])

        def w(name, a=0, n=None):
            c, width = WCOL[name]
            return W[:, c + a:c + a + (n if n is not None else width - a)]

        def v(name):
            return vec[:, VEC[name]:VEC[name] + 1]

        xin = two("xin", [128, 2, T])
        zsum = sb("zsum", [128, 2, T])
        dev = sb("dev", [128, 2, T])
        devsq = sb("devsq", [128, 2, T])
        var_a = sb("var_a", [128, 4])
        rstd_a = sb("rstd_a", [128, 4])
        nrm = sb("nrm", [128, 2, T])
        qn = two("qn", [128, T])
        kvn = sb("kvn", [128, T])
        parts = sb("parts", [128, 3, 2, T], BF16)
        left = sb("left", [128, 2, T])
        q_stack = two("q_stack", [128, H0 // 2, T], BF16)
        k_stack = two("k_stack", [128, H0 // 2, T], BF16)
        v_pad = two("v_pad", [128, 2, H0, 128])
        top = sb("top", [128, 2, H0])
        guard = sb("guard", [128, 2, 2, H0], BF16)
        guard_t = sb("guard_t", [2 * H0, T], BF16)
        probs = [sb(f"probs{n}", [128, 2, T]) for n in range(PROBS)]
        rden = sb("rden", [64, 2 * T])
        ctxn = sb("ctxn", [64, 2 * T])
        res = sb("res", [128, T])
        dev_h = sb("dev_h", [128, T])
        devsq_h = sb("devsq_h", [128, T])
        var_h = sb("var_h", [128, 2])
        rstd_h = sb("rstd_h", [128, 2])
        nrm_h = sb("nrm_h", [128, T])
        fn = sb("fn", [128, T])
        hid = sb("hid", [128, 2, T])
        x1 = two("x1", [128, E])
        prev = two("prev", [128, 2, 2])
        s0 = two("s0", [128, 2, S1])
        stats = sb("stats", [128, 6])
        mean_r = sb("mean_r", [128, 2])
        var_r = sb("var_r", [128, 1])
        rstd_r = sb("rstd_r", [128, 1])
        xh = sb("xh", [128, E])
        xt = sb("xt", [128, 2, NT + 1])
        sx = sb("sx", [128, 2, NT])
        xx = sb("xx", [128, 2, NT])
        th = sb("th", [128, 2, NT])
        mixed = sb("mixed", [128, 5, 2, NT])
        rk = sb("rk", [128, 2, 2, NT])
        vt = sb("vt", [128, 2, NT])
        v_rep = sb("v_rep", [128, 2, S1, NT])
        kv = v_rep
        dec1 = sb("dec1", [ND, NT])
        dec2 = sb("dec2", [128, 2, NT])
        dec = sb("dec", [128, 2, NT])
        st = sb("st", [128, 2, S1, NT])
        ruk = sb("ruk", [128, 2, NT])
        att = sb("att", [128, E])
        att2 = sb("att2", [128, E])
        attsq = sb("attsq", [128, E])
        attn = sb("attn", [128, E])
        hsum = sb("hsum", [128, H1])
        hvar = sb("hvar", [128, H1])
        hrs = sb("hrs", [128, H1])
        gate_t = sb("gate_t", [128, 2, NT])
        gate_h = sb("gate_h", [128, 2, NT])
        gate = sb("gate", [128, 2, NT])
        ag = sb("ag", [128, 2, NT])
        agg = sb("agg", [128, 2, NT])
        vtok = sb("vtok", [128, E])
        stats_o = sb("stats_o", [128, 6])
        mean_o = sb("mean_o", [128, 2])
        var_o = sb("var_o", [128, 1])
        rstd_o = sb("rstd_o", [128, 1])
        xh_o = sb("xh_o", [128, E])
        xt_o = sb("xt_o", [128, 2, NT + 1])
        sx_o = sb("sx_o", [128, 2, NT])
        x2 = sb("x2", [128, E])
        xkr = sb("xkr", [128, 2, 2, NT])
        kk = sb("kk", [128, 2, NT])
        kk2 = sb("kk2", [128, 2, NT])
        rr = sb("rr", [128, E])
        y = sb("y", [128, E])
        yo = two("yo", [128, E])

        stacks = nc.dram_tensor("stacks", (2, 2, C, PRODUCTS, T), BF16, kind="Internal").ap()
        values = nc.dram_tensor("values", (2, 2, 128, NT), F32, kind="Internal").ap()

        a_even, a_odd = psum("a_even"), psum("a_odd")
        h_even, h_odd, h_sum = psum("h_even"), psum("h_odd"), psum("h_sum")
        r_one, r_two = psum("r_one"), psum("r_two")
        o_bank = psum("o_bank")
        a_score, h_score = [a_even, a_odd], [h_even, h_odd]

        s_const, s_weights, s_setup, s_pads = (sem(n) for n in ("s_const", "s_weights", "s_setup", "s_pads"))
        s_x_in, s_prev_in, s_spilled, s_stacked, s_guard_in, s_v_out, s_v_rep, s_stored = (
            two_sems(n) for n in ("s_x_in", "s_prev_in", "s_spilled", "s_stacked", "s_guard_in", "s_v_out", "s_v_rep", "s_stored"))
        (s_zsum, s_centred, s_dev, s_var, s_vareps, s_rstd, s_spread, s_nrm, s_qkvn, s_qk, s_v, s_high, s_left, s_middle, s_parts,
         s_v_padded, s_scored, s_top, s_guard, s_guard_T, s_guard_c) = (sem("s_a_" + n) for n in (
             "zsum centred dev var vareps rstd spread nrm qkvn qk v high left middle parts "
             "v_padded scored top guard guard_T guard_c").split())
        (s_score_t, s_probs, s_sum, s_ctxn, s_wo, s_res, s_hcentred, s_hdev, s_hvar, s_hvareps, s_hrstd, s_hspread, s_hnrm, s_fn, s_ffn1,
         s_gelu, s_ffn2, s_x1) = (sem("s_h_" + n) for n in (
             "score_t probs sum ctxn wo res centred dev var vareps rstd spread nrm fn ffn1 gelu ffn2 x1").split())
        (s_var1, s_rstd1, s_xh1, s_xh1_T, s_xt1, s_xx1, s_maa1, s_tanh1, s_maa2, s_mix1, s_maa3, s_mixed, s_rk, s_vg, s_rk_sb, s_v_sb, s_gate, s_gated, s_dec1,
         s_dec1_sb, s_dec2, s_vtok, s_vtok_sb, s_dec, s_kv, s_st, s_rst_low, s_rst_high, s_ruk, s_att, s_hvareps1, s_hrs, s_attn, s_attn_T, s_ag, s_agg,
         s_wo1, s_var2, s_rstd2, s_xh2, s_xh2_T, s_xt2, s_xkr, s_ffkr, s_kk, s_sigm, s_ffv, s_done) = (sem("s_r_" + n) for n in (
             "var1 rstd1 xh1 xh1_T xt1 xx1 maa1 tanh1 maa2 mix1 maa3 mixed rk vg rk_sb v_sb gate gated dec1 dec1_sb dec2 vtok vtok_sb dec kv st rst_low rst_high "
             "ruk att hvareps hrs attn attn_T ag agg wo1 var2 rstd2 xh2 xh2_T xt2 xkr ffkr kk sigm ffv done").split())
        s_table = sem("s_table")
        s_guard_high, s_rden, s_norm1, s_edge1, s_sx1, s_mix5, s_decay, s_heads, s_norm2, s_edge2, s_x2, s_sx2, s_y, s_relu, s_hsum2 = (sem(n) for n in (
            "s_guard_high s_rden s_norm1 s_edge1 s_sx1 s_mix5 s_decay s_heads s_norm2 s_edge2 s_x2 s_sx2 s_y s_relu s_hsum2").split())

        def nth(batch, each, n):
            return batch.n * each + n

        def dma(batch, count=1):
            return batch.k * (16 * count) + 16 * count

        flat = lambda ap: ap.rearrange("p a t -> p (a t)")
        block = stack.enter_context(nc.Block())

        @block.sync
        def _(sp):
            sp.dma_start(W[:, 0:NW_A], weights[:, 0:NW_A]).then_inc(s_const, 16)
            sp.dma_start(vec[:, :], vecs).then_inc(s_const, 16)
            sp.dma_start(pe_tab[:, :], pos).then_inc(s_const, 16)

            def turn(a, g, h, r, o):
                if a:
                    if not (isinstance(a.n, int) and a.n < 2):
                        sp.wait_ge(s_zsum, a.n - 1)
                    sp.dma_start(xin[a.p][:, 0, :], x[bass.ds(a.n, 1), :, :].rearrange("a c t -> (a c) t")).then_inc(s_x_in[a.p], 16)
                    sp.dma_start(xin[a.p][:, 1, :], ctx_in[bass.ds(a.n, 1), :, :].rearrange("a c t -> (a c) t")).then_inc(s_x_in[a.p], 16)
                if g:
                    sp.wait_ge(s_guard_c, g.n + 1)
                    for part in range(2):
                        for e in range(2):
                            row = 64 * e + SCORE_ROWS + part
                            sp.dma_start(q_stack[g.p][row:row + 1, :, :], guard_t[part * H0 + e:part * H0 + H0:2, :]
                                         ).then_inc(s_guard_in[g.p], 16)
                if r:
                    sp.wait_ge(s_v_sb, r.n + 1)
                    sp.dma_start(values[r.p].rearrange("h p t -> p h t"), vt[:, :, :]).then_inc(s_v_out[r.p], 16)
                    sp.wait_ge(s_v_out[r.p], dma(r))
                    for half in range(2):
                        sp.dma_start(v_rep[:, half, :, :], values[r.p, half].rearrange("(g d) t -> g (d t)", d=S1)[:, None, :]
                                     .broadcast_to([16, S1, S1 * NT])).then_inc(s_v_rep[r.p], 16)
                if o:
                    sp.wait_ge(s_done, o.n + 2)
                    sp.dma_start(out[bass.ds(o.n, 1), :, :].rearrange("a l e -> (a l) e"), yo[o.p][:, :]).then_inc(s_stored[o.p], 16)
                if h:
                    if not (isinstance(h.n, int) and h.n < 2):
                        sp.wait_ge(s_done, h.n)
                    sp.dma_start(flat(prev[h.p][:, :, :]), first[bass.ds(h.n, 1), :, 0:4].rearrange("a p n -> (a p) n")).then_inc(s_prev_in[h.p], 16)
                    sp.dma_start(flat(s0[h.p][:, :, :]), first[bass.ds(h.n, 1), :, 4:20].rearrange("a p n -> (a p) n")).then_inc(s_prev_in[h.p], 16)
                if a:
                    for part in range(3):
                        sp.wait_ge((s_high, s_middle, s_parts)[part], a.n + 1)
                        for side, which in enumerate((Q_ROWS, K_ROWS)):
                            rows = which[part]
                            sp.dma_start(stacks[a.p, side, :, rows, :], parts[:, part, side, None, :].broadcast_to([128, len(range(PRODUCTS)[rows]), T])
                                         ).then_inc(s_spilled[a.p], 16)
                    if isinstance(a.n, int) and a.n == 0:
                        sp.wait_ge(s_setup, SETUP)
                    sp.wait_ge(s_spilled[a.p], dma(a, 6))
                    for side, dst in enumerate((q_stack, k_stack)):
                        for e in range(2):
                            sp.dma_start(dst[a.p][64 * e:64 * e + SCORE_ROWS, :, :],
                                         stacks[a.p, side].rearrange("(i e d) r t -> e (d r) i t", e=2, d=D0)[e]).then_inc(s_stacked[a.p], 16)

            turns(sp, turn)
            for p in range(2):
                sp.wait_ge(s_stored[p], 16 * (B // 2 + 1))

        @block.tensor
        def _(pe):
            pe.wait_ge(s_const, CONSTS)
            pe.wait_ge(s_setup, SETUP)
            ident = w("ident")

            def channelwise(dst, name, src):
                for m in range(2):
                    for half in range(2):
                        mm = pe.matmul(dst[:, m * 128:(m + 1) * 128], w(name, half * E + m * 128, 128), src[:, half, :],
                                       start=half == 0, stop=half == 1)
                return mm

            def tokenwise(dst, name, src):
                for half in range(2):
                    mm = pe.matmul(dst, src[:, half, :], w(name, half * E, E), start=half == 0, stop=half == 1)
                return mm

            def token_mix(group, dst):
                for half in range(2):
                    mm = pe.matmul(dst[:, half * 128:(half + 1) * 128], w(f"maa_w2_{group}", half * 128, 128), th[:, group // 4, :],
                                   start=True, stop=True)
                return mm

            def turn(a, g, h, r, o):
                if h and isinstance(h.n, int) and h.n == 0:
                    pe.wait_ge(s_weights, 16)
                for slot in range(SLOTS):
                    if h and slot in HEAD_SLOTS:
                        head = HEAD_SLOTS.index(slot)
                        if head == 0:
                            pe.wait_ge(s_guard_in[h.p], dma(h, 4))
                            if not (isinstance(h.n, int) and h.n == 0):
                                pe.wait_ge(s_x1, h.n)
                        if head >= 2:
                            pe.wait_ge(s_probs, h.n * H0 + head - 1)
                        e = 64 * (head % 2)
                        for j in range(2):
                            mm = pe.matmul(h_score[head % 2][:, j * T:(j + 1) * T],
                                           k_stack[h.p][e:e + GUARD_ROWS, head // 2, j * 128:(j + 1) * 128],
                                           q_stack[h.p][e:e + GUARD_ROWS, head // 2, :], start=True, stop=True)
                        mm.then_inc(s_score_t, 1)
                    if g and slot in G_SLOTS:
                        head = G_SLOTS.index(slot)
                        if head == 0:
                            pe.wait_ge(s_stacked[g.p], dma(g, 4))
                            pe.wait_ge(s_v_padded, g.n + 1)
                        if head >= 2:
                            pe.wait_ge(s_top, g.n * H0 + head - 1)
                        e = 64 * (head % 2)
                        for j in range(2):
                            mm = pe.matmul(a_score[head % 2][:, j * T:(j + 1) * T],
                                           q_stack[g.p][e:e + SCORE_ROWS, head // 2, j * 128:(j + 1) * 128],
                                           k_stack[g.p][e:e + SCORE_ROWS, head // 2, :], start=True, stop=True)
                        mm.then_inc(s_scored, 1)
                    if g and slot == G_GUARD:
                        pe.wait_ge(s_guard, g.n + 1)
                        for j in range(2):
                            mm = pe.matmul(a_even[0:2 * H0, j * 128:(j + 1) * 128], guard[:, j, :, :].rearrange("p a h -> p (a h)"),
                                           ident_bf[:, :], start=True, stop=True)
                        mm.then_inc(s_guard_T, 1)
                    if a and slot == A_CENTRE:
                        pe.wait_ge(s_zsum, a.n + 1)
                        if not (isinstance(a.n, int) and a.n == 0):
                            pe.wait_ge(s_guard_c, a.n)
                        pe.matmul(a_even[:, :], w("center"), flat(zsum[:, :, :]), start=True, stop=True).then_inc(s_centred, 1)
                    if a and slot == A_VAR:
                        pe.wait_ge(s_dev, a.n * 2 + 2)
                        for j in range(4):
                            mm = pe.matmul(a_odd[:, j:j + 1], devsq[:, j // 2, (j % 2) * 128:(j % 2) * 128 + 128], w("mean"),
                                           start=True, stop=True)
                        mm.then_inc(s_var, 1)
                    if a and slot == A_SPREAD:
                        pe.wait_ge(s_rstd, a.n + 1)
                        for j in range(4):
                            mm = pe.matmul(a_odd[:, j * 128:(j + 1) * 128], rstd_a[:, j:j + 1].broadcast_to([128, 128]), ident,
                                           start=True, stop=True)
                        mm.then_inc(s_spread, 1)
                    if a and slot == A_PROJECT:
                        pe.wait_ge(s_qkvn, a.n * 2 + 2)
                        pe.matmul(a_even[:, 0:T], w("Wq"), qn[a.p][:, :], start=True, stop=True)
                        pe.matmul(a_even[:, T:2 * T], w("Wk"), kvn[:, :], start=True, stop=True).then_inc(s_qk, 1)
                        for j in range(2):
                            mm = pe.matmul(a_odd[:, j * 128:(j + 1) * 128], kvn[:, j * 128:(j + 1) * 128], w("Wv"), start=True, stop=True)
                        mm.then_inc(s_v, 1)
                    if r and slot == R_TURN:
                        pe.wait_ge(s_xh1, r.n + 1)
                        if not (isinstance(r.n, int) and r.n == 0):
                            pe.wait_ge(s_vtok_sb, r.n)
                        for half in range(2):
                            mm = pe.transpose(r_one[:, half * 128:(half + 1) * 128], xh[:, half * 128:(half + 1) * 128], ident)
                        mm.then_inc(s_xh1_T, 1)
                    if r and slot == R_MAA1:
                        pe.wait_ge(s_xx1, r.n + 1)
                        for m, n in ((0, 128), (1, 32)):
                            for half in range(2):
                                mm = pe.matmul(r_two[0:n, m * 128:(m + 1) * 128], w("maa_w1", half * 160 + m * 128, n), xx[:, half, :],
                                               start=half == 0, stop=half == 1)
                        mm.then_inc(s_maa1, 1)
                    if r and slot == R_MAA2:
                        pe.wait_ge(s_tanh1, r.n * 2 + 2)
                        for group in range(2):
                            mm = token_mix(group, r_one[:, group * 256:(group + 1) * 256])
                        mm.then_inc(s_maa2, 1)
                        for group in range(2):
                            mm = token_mix(2 + group, r_two[:, group * 256:(group + 1) * 256])
                        mm.then_inc(s_maa2, 1)
                    if r and slot == R_MAA3:
                        pe.wait_ge(s_mix1, r.n + 1)
                        token_mix(4, r_one[:, 0:256]).then_inc(s_maa3, 1)
                    if r and slot == R_VG:
                        pe.wait_ge(s_mixed, r.n + 1)
                        channelwise(r_one[:, 0:E], "WvT", mixed[:, MIX_V])
                        channelwise(r_one[:, E:2 * E], "WgT", mixed[:, MIX_G]).then_inc(s_vg, 1)
                    if r and slot == R_RK:
                        channelwise(r_two[:, 0:E], "WrT", mixed[:, MIX_R])
                        channelwise(r_two[:, E:2 * E], "WkT", mixed[:, MIX_K]).then_inc(s_rk, 1)
                    if r and slot == R_DECAY:
                        pe.wait_ge(s_rk_sb, r.n + 1)
                        for half in range(2):
                            mm = pe.matmul(r_two[0:ND, 0:NT], w("decay_w1", half * ND, ND), mixed[:, MIX_W, half, :], start=half == 0, stop=half == 1)
                        mm.then_inc(s_dec1, 1)
                    if r and slot == R_DECAY2:
                        pe.wait_ge(s_dec1_sb, r.n + 1)
                        for m in range(2):
                            mm = pe.matmul(r_two[:, 128 + m * 128:128 + (m + 1) * 128], w("decay_w2", m * 128, 128)[0:ND, :], dec1[:, :],
                                           start=True, stop=True)
                        mm.then_inc(s_dec2, 1)
                    if r and slot == R_OWN:
                        pe.wait_ge(s_gate, r.n * 2 + 2)
                        for half in range(2):
                            mm = pe.transpose(r_one[:, half * 128:(half + 1) * 128], vt[:, half, :], ident)
                        mm.then_inc(s_vtok, 1)
                    if o and slot in O_ATTEND_SLOTS:
                        half, quarter = divmod(O_ATTEND_SLOTS.index(slot), 2)
                        if half == 0 and quarter == 0:
                            pe.wait_ge(s_ruk, o.n + 1)
                            pe.wait_ge(s_done, o.n + 1)
                            for side in range(2):
                                pe.matmul(o_bank[:, E + side * 16:E + side * 16 + 16], ruk[:, side, :], w("heads"), start=True, stop=True)
                            pe.wait_ge(s_rst_low, o.n + 1)
                        if half == 1 and quarter == 0:
                            pe.wait_ge(s_rst_high, o.n + 1)
                        for d in range(quarter * S1 // 2, (quarter + 1) * S1 // 2):
                            mm = pe.matmul(o_bank[:, (half * S1 + d) * 16:(half * S1 + d + 1) * 16], st[:, half, d, :], w("heads"),
                                           start=True, stop=True)
                        if half == 1 and quarter == 1:
                            mm.then_inc(s_att, 1)
                    if o and slot == O_TURN_ATT:
                        pe.wait_ge(s_attn, o.n + 1)
                        for half in range(2):
                            mm = pe.transpose(o_bank[:, half * 128:(half + 1) * 128], attn[:, half * 128:(half + 1) * 128], ident)
                        mm.then_inc(s_attn_T, 1)
                    if o and slot == O_WO:
                        pe.wait_ge(s_agg, o.n + 1)
                        tokenwise(o_bank[:, 0:E], "WoT", agg).then_inc(s_wo1, 1)
                    if o and slot == O_TURN2:
                        pe.wait_ge(s_xh2, o.n + 1)
                        for half in range(2):
                            mm = pe.transpose(o_bank[:, half * 128:(half + 1) * 128], xh_o[:, half * 128:(half + 1) * 128], ident)
                        mm.then_inc(s_xh2_T, 1)
                    if o and slot == O_FF_IN:
                        pe.wait_ge(s_xkr, o.n + 1)
                        channelwise(o_bank[:, 0:E], "FkT", xkr[:, 0])
                        tokenwise(o_bank[:, E:2 * E], "FrT", xkr[:, 1]).then_inc(s_ffkr, 1)
                    if o and slot == O_FF_OUT:
                        pe.wait_ge(s_kk, o.n + 1)
                        pe.wait_ge(s_sigm, o.n + 1)
                        tokenwise(o_bank[:, 0:E], "FvT", kk2).then_inc(s_ffv, 1)

                    if h and slot in HEAD_SUM_SLOTS:
                        head = HEAD_SUM_SLOTS.index(slot)
                        pe.wait_ge(s_probs, h.n * H0 + head + 1)
                        for j in range(2):
                            mm = pe.matmul(h_sum[:, (head // 8) * T:(head // 8 + 1) * T], v_pad[h.p][:, j, head, :], probs[head % PROBS][:, j, :],
                                           start=(head % 8 == 0 and j == 0), stop=(head % 8 == 7 and j == 1))
                        mm.then_inc(s_sum, 1)
                    if h and slot == H_WO:
                        pe.wait_ge(s_ctxn, nth(h, 2, 2))
                        for half in range(2):
                            mm = pe.matmul(h_even[:, 0:T], w("Wo", half * C, C)[0:64, :], ctxn[:, half * T:(half + 1) * T], start=half == 0, stop=half == 1)
                        mm.then_inc(s_wo, 1)
                    if h and slot == H_CENTRE:
                        pe.wait_ge(s_res, h.n + 1)
                        pe.matmul(h_odd[:, 0:T], w("center"), res[:, :], start=True, stop=True).then_inc(s_hcentred, 1)
                    if h and slot == H_VAR:
                        pe.wait_ge(s_hdev, h.n * 2 + 2)
                        for j in range(2):
                            mm = pe.matmul(h_sum[:, j:j + 1], devsq_h[:, j * 128:(j + 1) * 128], w("mean"), start=True, stop=True)
                        mm.then_inc(s_hvar, 1)
                    if h and slot == H_SPREAD:
                        pe.wait_ge(s_hrstd, h.n + 1)
                        for j in range(2):
                            mm = pe.matmul(h_odd[:, j * 128:(j + 1) * 128], rstd_h[:, j:j + 1].broadcast_to([128, 128]), ident, start=True, stop=True)
                        mm.then_inc(s_hspread, 1)
                    if h and slot == H_FFN1:
                        pe.wait_ge(s_fn, h.n + 1)
                        for m in range(2):
                            mm = pe.matmul(h_even[:, m * T:(m + 1) * T], w("W1", m * 128, 128), fn[:, :], start=True, stop=True)
                        mm.then_inc(s_ffn1, 1)
                    if h and slot == H_FFN2:
                        pe.wait_ge(s_gelu, h.n + 1)
                        for m in range(2):
                            mm = pe.matmul(h_sum[:, 0:T], w("W2", m * 128, 128), hid[:, m, :], start=m == 0, stop=m == 1)
                        mm.then_inc(s_ffn2, 1)

            turns(pe, turn)

        @block.scalar
        def _(act):
            act.wait_ge(s_x_in[0], 32)
            act.dma_start(W[:, NW_A:NW], weights[:, NW_A:NW]).then_inc(s_weights, 16)
            act.wait_ge(s_const, CONSTS)
            act.wait_ge(s_pads, PADS)

            def turn(a, g, h, r, o):
                for slot in range(SLOTS):
                    if h and slot in HEAD_SLOTS:
                        head = HEAD_SLOTS.index(slot)
                        act.wait_ge(s_score_t, h.n * H0 + head + 1)
                        if head >= PROBS:
                            act.wait_ge(s_sum, h.n * H0 + head - PROBS + 1)
                        act.activation(flat(probs[head % PROBS][:, :, :]), h_score[head % 2][:, :], ACT.Exp, scale=SCORE_SCALE).then_inc(s_probs, 1)
                    if a and slot == A_CENTRE:
                        act.wait_ge(s_centred, a.n + 1)
                        act.activation(flat(devsq[:, :, :]), a_even[:, :], ACT.Square).then_inc(s_dev, 1)
                        act.activation(flat(dev[:, :, :]), a_even[:, :], ACT.Copy).then_inc(s_dev, 1)
                    if a and slot == A_AFFINE:
                        act.wait_ge(s_nrm, a.n + 1)
                        if not (isinstance(a.n, int) and a.n < 2):
                            act.wait_ge(s_res, a.n - 1)
                        act.activation(qn[a.p][:, :], nrm[:, 0, :], ACT.Identity, scale=v("ln_q_g"), bias=v("ln_q_b")).then_inc(s_qkvn, 1)
                        act.activation(kvn[:, :], nrm[:, 1, :], ACT.Identity, scale=v("ln_kv_g"), bias=v("ln_kv_b")).then_inc(s_qkvn, 1)
                    if a and slot == A_PARTS:
                        act.wait_ge(s_qk, a.n + 1)
                        act.activation(parts[:, 0].rearrange("p s t -> p (s t)"), a_even[:, :], ACT.Copy).then_inc(s_high, 1)
                        act.wait_ge(s_v, a.n + 1)
                        if not (isinstance(a.n, int) and a.n < 2):
                            act.wait_ge(s_sum, (a.n - 1) * H0)
                        for j in range(2):
                            for s in range(2):
                                ins = act.activation(diag(v_pad[a.p], j, s), a_odd[:, j * 128 + s * 64:j * 128 + s * 64 + 64]
                                                     .rearrange("p (g d) -> p g d", d=D0), ACT.Copy)
                        ins.then_inc(s_v_padded, 1)
                        act.wait_ge(s_left, a.n + 1)
                        act.activation(parts[:, 1].rearrange("p s t -> p (s t)"), flat(left[:, :, :]), ACT.Copy).then_inc(s_middle, 1)
                    if g and slot == G_GUARD:
                        act.wait_ge(s_guard_T, g.n + 1)
                        act.activation(guard_t[:, :], a_even[0:2 * H0, 0:T], ACT.Copy).then_inc(s_guard_c, 1)

                    if r and slot == R_TURN:
                        act.wait_ge(s_xh1_T, r.n + 1)
                        for half in range(2):
                            ins = act.activation(xt[:, half, 1:NT + 1], r_one[:, half * 128:(half + 1) * 128], ACT.Identity,
                                                 scale=v(f"ln1_w_{half}"), bias=v(f"ln1_b_{half}"))
                        ins.then_inc(s_xt1, 1)
                    if r and slot == R_MAA1:
                        act.wait_ge(s_maa1, r.n + 1)
                        act.activation(th[:, 0, :], r_two[:, 0:128], ACT.Tanh).then_inc(s_tanh1, 1)
                        act.activation(th[0:32, 1, :], r_two[0:32, 128:256], ACT.Tanh).then_inc(s_tanh1, 1)
                    if r and slot == R_VG:
                        act.wait_ge(s_vg, r.n + 1)
                        act.activation(flat(vt[:, :, :]), r_one[:, 0:E], ACT.Copy).then_inc(s_v_sb, 1)
                        act.activation(flat(gate_t[:, :, :]), r_one[:, E:2 * E], ACT.Tanh, scale=0.5).then_inc(s_gate, 1)
                        act.activation(flat(gate_h[:, :, :]), r_one[:, E:2 * E], ACT.Copy, scale=0.5).then_inc(s_gate, 1)
                    if r and slot == R_RK:
                        act.wait_ge(s_rk, r.n + 1)
                        act.activation(rk[:, :, :, :].rearrange("p a b t -> p (a b t)"), r_two[:, :], ACT.Copy).then_inc(s_rk_sb, 1)
                    if r and slot == R_DECAY:
                        act.wait_ge(s_dec1, r.n + 1)
                        act.activation(dec1[:, :], r_two[0:ND, 0:NT], ACT.Tanh).then_inc(s_dec1_sb, 1)
                    if r and slot == R_DECAY2:
                        act.wait_ge(s_dec2, r.n + 1)
                        for m in range(2):
                            ins = act.activation(dec2[:, m, :], r_two[:, 128 + m * 128:128 + (m + 1) * 128], ACT.Exp, bias=v(f"decay_{m}"))
                        ins.then_inc(s_decay, 1)
                        act.wait_ge(s_decay, r.n + 1)
                        act.activation(flat(dec[:, :, :]), flat(dec2[:, :, :]), ACT.Exp, scale=-1.0).then_inc(s_dec, 1)
                    if r and slot == R_OWN:
                        act.wait_ge(s_vtok, r.n + 1)
                        if not (isinstance(r.n, int) and r.n == 0):
                            act.wait_ge(s_hvareps1, r.n)
                        act.activation(vtok[:, :], r_one[:, 0:E], ACT.Copy).then_inc(s_vtok_sb, 1)
                    if o and slot == O_TURN_ATT:
                        act.wait_ge(s_attn_T, o.n + 1)
                        for half in range(2):
                            ins = act.activation(ag[:, half, :], o_bank[:, half * 128:(half + 1) * 128], ACT.Identity,
                                                 scale=v(f"gn_w_{half}"), bias=v(f"gn_b_{half}"))
                        ins.then_inc(s_ag, 1)
                    if o and slot == O_TURN2:
                        act.wait_ge(s_xh2_T, o.n + 1)
                        for half in range(2):
                            ins = act.activation(xt_o[:, half, 1:NT + 1], o_bank[:, half * 128:(half + 1) * 128], ACT.Identity,
                                                 scale=v(f"ln2_w_{half}"), bias=v(f"ln2_b_{half}"))
                        ins.then_inc(s_xt2, 1)
                    if o and slot == O_FF_IN:
                        act.wait_ge(s_ffkr, o.n + 1)
                        act.activation(flat(kk[:, :, :]), o_bank[:, 0:E], ACT.Relu).then_inc(s_relu, 1)
                        act.wait_ge(s_relu, o.n + 1)
                        act.activation(flat(kk2[:, :, :]), flat(kk[:, :, :]), ACT.Square).then_inc(s_kk, 1)
                        act.activation(rr[:, :], o_bank[:, E:2 * E], ACT.Tanh, scale=0.5).then_inc(s_sigm, 1)

                    if h and slot == H_CENTRE:
                        act.wait_ge(s_hcentred, h.n + 1)
                        act.activation(devsq_h[:, :], h_odd[:, 0:T], ACT.Square).then_inc(s_hdev, 1)
                        act.activation(dev_h[:, :], h_odd[:, 0:T], ACT.Copy).then_inc(s_hdev, 1)
                    if h and slot == H_SPREAD:
                        act.wait_ge(s_hnrm, h.n + 1)
                        act.activation(fn[:, :], nrm_h[:, :], ACT.Identity, scale=v("ffn_g"), bias=v("ffn_b")).then_inc(s_fn, 1)
                    if h and slot == TO_GELU:
                        if not (isinstance(h.n, int) and h.n == 0):
                            act.wait_ge(s_table, nth(h, 2, 0))
                        act.activation(table_out[:, :], vec[:, 0:1], ACT.Gelu).then_inc(s_table, 1)
                    if h and slot == H_FFN1:
                        act.wait_ge(s_ffn1, h.n + 1)
                        for m in range(2):
                            ins = act.activation(hid[:, m, :], h_even[:, m * T:(m + 1) * T], ACT.Gelu, bias=v(f"b1_{m}"))
                        ins.then_inc(s_gelu, 1)
                    if h and slot == TO_EXP:
                        act.wait_ge(s_table, nth(h, 2, 1))
                        act.activation(table_out[:, :], vec[:, 0:1], ACT.Exp, scale=0.0).then_inc(s_table, 1)

            turns(act, turn)

        @block.gpsimd
        def _(pool):
            pool.memset(mhalf[:, :], -0.5).then_inc(s_setup, 1)
            pool.memset(th[:, :, :], 0.0).then_inc(s_setup, 1)
            for p in range(2):
                pool.memset(k_stack[p][:, :, :], 1.0).then_inc(s_setup, 1)
                pool.memset(yo[p][:, 0:1], 0.0).then_inc(s_stored[p], 16)
            pool.memset(x2[:, 0:1], 0.0).then_inc(s_done, 1)
            pool.wait_ge(s_const, CONSTS)
            pool.tensor_copy(ident_bf[:, :], w("ident")).then_inc(s_setup, 1)
            pool.wait_ge(s_setup, SETUP)

            def turn(a, g, h, r, o):
                for slot in range(SLOTS):
                    if a and slot == A_CENTRE:
                        pool.wait_ge(s_x_in[a.p], dma(a, 2))
                        if not (isinstance(a.n, int) and a.n == 0):
                            pool.wait_ge(s_spilled[1 - a.p], (a.k + (a.p - 1)) * 96 + 96)
                            pool.wait_ge(s_v_padded, a.n)
                        pool.tensor_tensor(zsum[:, :, :], xin[a.p][:, :, :], pe_tab[:, None, :].broadcast_to([128, 2, T]), ALU.add).then_inc(s_zsum, 1)
                    if a and slot == A_VAR:
                        pool.wait_ge(s_vareps, a.n + 1)
                        pool.tensor_tensor(rstd_a[:, :], var_a[:, :], mhalf[:, 0:4], ALU.pow).then_inc(s_rstd, 1)
                    if r and slot == R_EPS:
                        pool.wait_ge(s_var1, r.n + 1)
                        pool.tensor_tensor(rstd_r[:, :], var_r[:, :], mhalf[:, 0:1], ALU.pow).then_inc(s_rstd1, 1)
                    if r and slot == R_KV:
                        pool.wait_ge(s_v_rep[r.p], dma(r, 2))
                        pool.wait_ge(s_rk_sb, r.n + 1)
                        for half in range(2):
                            pool.tensor_tensor(kv[:, half, :, :], v_rep[:, half, :, :], rk[:, 1, half, None, :].broadcast_to([128, S1, NT]), ALU.mult
                                               ).then_inc(s_kv, 1)
                    if r and slot == R_READ:
                        pool.wait_ge(s_st, r.n * 2 + 1)
                        pool.tensor_tensor(st[:, 0, :, :], st[:, 0, :, :], rk[:, 0, 0, None, :].broadcast_to([128, S1, NT]), ALU.mult).then_inc(s_rst_low, 1)
                    if o and slot == O_HEADS_SLOTS[5]:
                        pool.wait_ge(s_hvareps1, o.n + 1)
                        pool.tensor_tensor(hrs[:, :], hvar[:, :], mhalf[:, :], ALU.pow).then_inc(s_hrs, 1)
                    if o and slot == O_EPS:
                        pool.wait_ge(s_var2, o.n + 1)
                        pool.tensor_tensor(rstd_o[:, :], var_o[:, :], mhalf[:, 0:1], ALU.pow).then_inc(s_rstd2, 1)
                    if h and slot == H_VAR:
                        pool.wait_ge(s_hvareps, h.n + 1)
                        pool.tensor_tensor(rstd_h[:, :], var_h[:, :], mhalf[:, 0:2], ALU.pow).then_inc(s_hrstd, 1)

            turns(pool, turn)

        @block.vector
        def _(dve):
            for p in range(2):
                dve.memset(v_pad[p][:, :, :, :], 0.0).then_inc(s_pads, 1)
            dve.wait_ge(s_pads, 2)
            for p in range(2):
                for j in range(2):
                    for half in range(2):
                        dve.memset(diag(v_pad[p], j, half, 64), 1.0).then_inc(s_pads, 1)
            dve.wait_ge(s_const, CONSTS)
            heads = lambda ap: ap.rearrange("p (h d) -> p h d", d=S1)
            every_d = lambda ap: ap[:, :, None].broadcast_to([128, H1, S1])

            def turn(a, g, h, r, o):
                for slot in range(SLOTS):
                    if g and slot in G_SLOTS:
                        head = G_SLOTS.index(slot)
                        dve.wait_ge(s_scored, g.n * H0 + head + 1)
                        dve.tensor_reduce(top[:, :, head], a_score[head % 2][:, :].rearrange("p (a t) -> p a t", a=2), AX.X, ALU.max
                                          ).then_inc(s_top, 1)
                        if head == H0 - 1:
                            dve.wait_ge(s_top, g.n * H0 + H0)
                            dve.tensor_scalar(guard[:, :, 0, :], top[:, :, :], -1.0, None, ALU.mult).then_inc(s_guard_high, 1)
                            dve.wait_ge(s_guard_high, g.n + 1)
                            dve.scalar_tensor_tensor(out=guard[:, :, 1, :], in0=top[:, :, :], scalar=-1.0, in1=guard[:, :, 0, :],
                                                     op0=ALU.mult, op1=ALU.subtract).then_inc(s_guard, 1)
                    if a and slot == A_VAR:
                        dve.wait_ge(s_var, a.n + 1)
                        dve.tensor_scalar(var_a[:, :], a_odd[:, 0:4], EPS, None, ALU.add).then_inc(s_vareps, 1)
                    if a and slot == A_SPREAD:
                        dve.wait_ge(s_spread, a.n + 1)
                        dve.tensor_tensor(flat(nrm[:, :, :]), a_odd[:, :], flat(dev[:, :, :]), ALU.mult).then_inc(s_nrm, 1)
                    if a and slot == A_PARTS:
                        dve.wait_ge(s_high, a.n + 1)
                        dve.tensor_tensor(flat(left[:, :, :]), a_even[:, :], parts[:, 0].rearrange("p s t -> p (s t)"), ALU.subtract).then_inc(s_left, 1)
                        dve.wait_ge(s_middle, a.n + 1)
                        dve.tensor_tensor(parts[:, 2], left[:, :, :], parts[:, 1], ALU.subtract).then_inc(s_parts, 1)
                    if r and slot == R_NORM:
                        dve.wait_ge(s_x1, r.n + 1)
                        if not (isinstance(r.n, int) and r.n == 0):
                            dve.wait_ge(s_rst_low, r.n)
                            dve.wait_ge(s_rst_high, r.n)
                        dve.bn_stats(stats[:, :], x1[r.p][:, :]).then_inc(s_norm1, 1)
                    if r and slot == R_AGGR:
                        dve.wait_ge(s_norm1, nth(r, 2, 1))
                        dve.wait_ge(s_prev_in[r.p], dma(r, 2))
                        dve.tensor_copy(xt[:, :, 0], prev[r.p][:, :, 1]).then_inc(s_edge1, 1)
                        dve.bn_aggr(mean_r[:, :], stats[:, :]).then_inc(s_norm1, 1)
                    if r and slot == R_EPS:
                        dve.wait_ge(s_norm1, nth(r, 2, 2))
                        dve.tensor_scalar(var_r[:, :], mean_r[:, 1:2], EPS, None, ALU.add).then_inc(s_var1, 1)
                    if r and slot == R_XH:
                        dve.wait_ge(s_rstd1, r.n + 1)
                        dve.tensor_scalar(xh[:, :], x1[r.p][:, :], mean_r[:, 0:1], rstd_r[:, :], ALU.subtract, ALU.mult).then_inc(s_xh1, 1)
                    if r and slot == R_TURN:
                        dve.wait_ge(s_xt1, r.n + 1)
                        dve.wait_ge(s_edge1, r.n + 1)
                        dve.tensor_tensor(sx[:, :, :], xt[:, :, 0:NT], xt[:, :, 1:NT + 1], ALU.subtract).then_inc(s_sx1, 1)
                        dve.wait_ge(s_sx1, r.n + 1)
                        for half in range(2):
                            ins = dve.scalar_tensor_tensor(out=xx[:, half, :], in0=sx[:, half, :], scalar=v(f"maa_x_{half}"), in1=xt[:, half, 1:NT + 1],
                                                           op0=ALU.mult, op1=ALU.add)
                        ins.then_inc(s_xx1, 1)
                    for group in range(5):
                        if r and slot == (R_MIX, R_MIX, R_MIX2, R_MIX2, R_MIX3)[group]:
                            if group == 0:
                                dve.wait_ge(s_maa2, r.n * 2 + 1)
                            if group == 2:
                                dve.wait_ge(s_maa2, r.n * 2 + 2)
                            if group == 4:
                                dve.wait_ge(s_maa3, r.n + 1)
                            src = (r_one, r_one, r_two, r_two, r_one)[group]
                            for half in range(2):
                                col = (group % 2) * 256 + half * 128 if group < 4 else half * 128
                                ins = dve.scalar_tensor_tensor(out=mixed[:, group, half, :], in0=src[:, col:col + 128], scalar=v(f"stack{group}_{half}"),
                                                               in1=sx[:, half, :], op0=ALU.add, op1=ALU.mult)
                            if group == 1:
                                ins.then_inc(s_mix1, 1)
                            if group == 4:
                                ins.then_inc(s_mix5, 1)
                    if r and slot == R_MIXED:
                        dve.wait_ge(s_mix5, r.n + 1)
                        for half in range(2):
                            ins = dve.tensor_tensor(mixed[:, :, half, :], mixed[:, :, half, :], xt[:, half, None, 1:NT + 1].broadcast_to([128, 5, NT]), ALU.add)
                        ins.then_inc(s_mixed, 1)
                    if r and slot == R_DECAY2:
                        dve.wait_ge(s_rk_sb, r.n + 1)
                        if not (isinstance(r.n, int) and r.n == 0):
                            dve.wait_ge(s_att, r.n)
                            dve.wait_ge(s_agg, r.n)
                        for half in range(2):
                            ins = dve.scalar_tensor_tensor(out=ruk[:, half, :], in0=rk[:, 0, half, :], scalar=v(f"faaaa_{half}"), in1=rk[:, 1, half, :],
                                                           op0=ALU.mult, op1=ALU.mult)
                        ins.then_inc(s_ruk, 1)
                        dve.wait_ge(s_gate, r.n * 2 + 2)
                        dve.scalar_tensor_tensor(out=flat(gate[:, :, :]), in0=flat(gate_t[:, :, :]), scalar=1.0, in1=flat(gate_h[:, :, :]),
                                                 op0=ALU.add, op1=ALU.mult).then_inc(s_gated, 1)
                    if r and slot in R_SCAN_SLOTS:
                        half, quarter = divmod(R_SCAN_SLOTS.index(slot), 2)
                        if quarter == 0:
                            dve.wait_ge(s_kv, r.n * 2 + half + 1)
                            dve.wait_ge(s_dec, r.n + 1)
                            if not (isinstance(r.n, int) and r.n == 0):
                                dve.wait_ge(s_att, r.n)
                            dve.tensor_copy(st[:, half, :, 0], s0[r.p][:, half, :])
                        for d in range(quarter * S1 // 2, (quarter + 1) * S1 // 2):
                            ins = dve.tensor_tensor_scan(st[:, half, d, 1:NT], dec[:, half, 0:NT - 1], kv[:, half, d, 0:NT - 1],
                                                         s0[r.p][:, half, d:d + 1], ALU.mult, ALU.add)
                        if quarter == 1:
                            ins.then_inc(s_st, 1)
                    if r and slot == R_READ:
                        dve.wait_ge(s_st, r.n * 2 + 2)
                        dve.tensor_tensor(st[:, 1, :, :], st[:, 1, :, :], rk[:, 0, 1, None, :].broadcast_to([128, S1, NT]), ALU.mult).then_inc(s_rst_high, 1)
                    for step in range(6):
                        if o and slot == O_HEADS_SLOTS[step]:
                            if step == 0:
                                dve.wait_ge(s_att, o.n + 1)
                                dve.wait_ge(s_vtok_sb, o.n + 1)
                                dve.tensor_tensor(heads(att2[:, :]), heads(vtok[:, :]), every_d(o_bank[:, E:E + H1]), ALU.mult).then_inc(s_heads, 1)
                            if step == 1:
                                dve.wait_ge(s_heads, nth(o, 5, 1))
                                for half in range(2):
                                    ins = dve.tensor_tensor(heads(att[:, half * 128:(half + 1) * 128]),
                                                            o_bank[:, half * 128:(half + 1) * 128].rearrange("p (d g) -> p g d", g=16),
                                                            heads(att2[:, half * 128:(half + 1) * 128]), ALU.add)
                                ins.then_inc(s_heads, 1)
                            if step == 2:
                                dve.wait_ge(s_heads, nth(o, 5, 2))
                                dve.tensor_reduce(hsum[:, :], heads(att[:, :]), AX.X, ALU.add).then_inc(s_heads, 1)
                            if step == 3:
                                dve.wait_ge(s_heads, nth(o, 5, 3))
                                dve.scalar_tensor_tensor(out=heads(att2[:, :]), in0=every_d(hsum[:, :]), scalar=-1.0 / S1, in1=heads(att[:, :]),
                                                         op0=ALU.mult, op1=ALU.add).then_inc(s_heads, 1)
                            if step == 4:
                                dve.wait_ge(s_heads, nth(o, 5, 4))
                                dve.tensor_tensor(attsq[:, :], att2[:, :], att2[:, :], ALU.mult).then_inc(s_heads, 1)
                            if step == 5:
                                dve.wait_ge(s_heads, nth(o, 5, 5))
                                dve.tensor_reduce(hsum[:, :], heads(attsq[:, :]), AX.X, ALU.add).then_inc(s_hsum2, 1)
                                dve.wait_ge(s_hsum2, o.n + 1)
                                dve.tensor_scalar(hvar[:, :], hsum[:, :], 1.0 / S1, EPS, ALU.mult, ALU.add).then_inc(s_hvareps1, 1)
                    if o and slot == O_TURN_ATT:
                        dve.wait_ge(s_hrs, o.n + 1)
                        dve.tensor_tensor(heads(attn[:, :]), heads(att2[:, :]), every_d(hrs[:, :]), ALU.mult).then_inc(s_attn, 1)
                    if o and slot == O_AG:
                        dve.wait_ge(s_ag, o.n + 1)
                        dve.wait_ge(s_gated, o.n + 1)
                        dve.tensor_tensor(agg[:, :, :], ag[:, :, :], gate[:, :, :], ALU.mult).then_inc(s_agg, 1)
                    if o and slot == O_WO:
                        dve.wait_ge(s_wo1, o.n + 1)
                        dve.tensor_tensor(x2[:, :], o_bank[:, 0:E], x1[o.p][:, :], ALU.add).then_inc(s_x2, 1)
                    if o and slot == O_NORM:
                        dve.wait_ge(s_x2, o.n + 1)
                        dve.bn_stats(stats_o[:, :], x2[:, :]).then_inc(s_norm2, 1)
                    if o and slot == O_AGGR:
                        dve.wait_ge(s_norm2, nth(o, 2, 1))
                        dve.tensor_copy(xt_o[:, :, 0], prev[o.p][:, :, 0]).then_inc(s_edge2, 1)
                        dve.bn_aggr(mean_o[:, :], stats_o[:, :]).then_inc(s_norm2, 1)
                    if o and slot == O_EPS:
                        dve.wait_ge(s_norm2, nth(o, 2, 2))
                        dve.tensor_scalar(var_o[:, :], mean_o[:, 1:2], EPS, None, ALU.add).then_inc(s_var2, 1)
                    if o and slot == O_XH:
                        dve.wait_ge(s_rstd2, o.n + 1)
                        dve.tensor_scalar(xh_o[:, :], x2[:, :], mean_o[:, 0:1], rstd_o[:, :], ALU.subtract, ALU.mult).then_inc(s_xh2, 1)
                    if o and slot == O_TURN2:
                        dve.wait_ge(s_xt2, o.n + 1)
                        dve.wait_ge(s_edge2, o.n + 1)
                        dve.tensor_tensor(sx_o[:, :, :], xt_o[:, :, 0:NT], xt_o[:, :, 1:NT + 1], ALU.subtract).then_inc(s_sx2, 1)
                        dve.wait_ge(s_sx2, o.n + 1)
                        for m, name in enumerate(("ffn_k", "ffn_r")):
                            for half in range(2):
                                ins = dve.scalar_tensor_tensor(out=xkr[:, m, half, :], in0=sx_o[:, half, :], scalar=v(f"{name}_{half}"),
                                                               in1=xt_o[:, half, 1:NT + 1], op0=ALU.mult, op1=ALU.add)
                        ins.then_inc(s_xkr, 1)
                    if o and slot == O_FF_OUT:
                        dve.wait_ge(s_ffv, o.n + 1)
                        dve.wait_ge(s_sigm, o.n + 1)
                        dve.scalar_tensor_tensor(out=y[:, :], in0=rr[:, :], scalar=1.0, in1=o_bank[:, 0:E], op0=ALU.add, op1=ALU.mult).then_inc(s_y, 1)
                        dve.wait_ge(s_y, o.n + 1)
                        dve.wait_ge(s_stored[o.p], dma(o))
                        dve.scalar_tensor_tensor(out=yo[o.p][:, :], in0=y[:, :], scalar=0.5, in1=x2[:, :], op0=ALU.mult, op1=ALU.add).then_inc(s_done, 1)

                    for half in range(2):
                        if h and slot == (H_CTX_LOW, H_CTX)[half]:
                            dve.wait_ge(s_sum, nth(h, H0, H0))
                            dve.reciprocal(rden[:, half * T:(half + 1) * T], h_sum[64:128, half * T:(half + 1) * T]).then_inc(s_rden, 1)
                            dve.wait_ge(s_rden, nth(h, 2, half + 1))
                            dve.tensor_tensor(ctxn[:, half * T:(half + 1) * T], h_sum[0:64, half * T:(half + 1) * T], rden[:, half * T:(half + 1) * T], ALU.mult
                                              ).then_inc(s_ctxn, 1)
                    if h and slot == H_WO:
                        dve.wait_ge(s_wo, h.n + 1)
                        dve.tensor_tensor(res[:, :], h_even[:, 0:T], qn[h.p][:, :], ALU.add).then_inc(s_res, 1)
                    if h and slot == H_VAR:
                        dve.wait_ge(s_hvar, h.n + 1)
                        dve.tensor_scalar(var_h[:, :], h_sum[:, 0:2], EPS, None, ALU.add).then_inc(s_hvareps, 1)
                    if h and slot == H_SPREAD:
                        dve.wait_ge(s_hspread, h.n + 1)
                        dve.tensor_tensor(nrm_h[:, :], h_odd[:, 0:T], dev_h[:, :], ALU.mult).then_inc(s_hnrm, 1)
                    if h and slot == H_FFN2:
                        dve.wait_ge(s_ffn2, h.n + 1)
                        if not (isinstance(h.n, int) and h.n < 2):
                            dve.wait_ge(s_done, h.n)
                        dve.scalar_tensor_tensor(out=x1[h.p][:, :], in0=h_sum[:, 0:T], scalar=v("b2"), in1=res[:, :], op0=ALU.add, op1=ALU.add
                                                 ).then_inc(s_x1, 1)

            turns(dve, turn)


PROBS = 3
SETUP = 5
CONSTS = 16 * 3
PADS = 2 + 8


def diag(v_pad, j, s, at=0):
    ap = v_pad[:, j, s * 8:(s + 1) * 8, at:at + D0]
    dims = [list(d) for d in ap.ap]
    dims[1][0] += D0
    return bass.AP(tensor=ap.tensor, offset=ap.offset, ap=dims)


def kernel(**inputs):
    import concourse.bacc as bacc
    from concourse.bass_utils import run_bass_kernel_spmd as run

    f = {k: np.asarray(a) for k, a in inputs.items()}
    L0 = {k[len("L0_xattn_"):]: a for k, a in f.items() if k.startswith("L0_")}
    L1 = {k[len("L1_xattn_"):]: a for k, a in f.items() if k.startswith("L1_")}

    def tiles(a, k=128):
        n = a.shape[0] // k
        return np.ascontiguousarray(a.reshape(n, k, -1).transpose(1, 0, 2)).reshape(k, -1)

    W = np.zeros((128, NW), np.float32)

    def put(name, a):
        c, width = WCOL[name]
        assert a.shape[1] == width, (name, a.shape, width)
        W[:a.shape[0], c:c + width] = a

    eye = np.eye(128, dtype=np.float32)
    put("center", eye - np.float32(1.0 / C))
    put("ident", eye)
    put("mean", np.full((128, 1), 1.0 / C, np.float32))
    put("heads", (np.arange(128)[:, None] // S1 == np.arange(16)[None, :]).astype(np.float32))
    for n in ("Wq", "Wk", "Wv"):
        put(n, L0[n])
    put("W1", L0["W1"])
    put("W2", tiles(L0["W2"]))
    put("Wo", tiles(L0["Wo"], 64))
    put("maa_w1", tiles(L1["maa_w1"]))
    for g in range(5):
        a = np.zeros((128, E), np.float32)
        a[32 * (g % 4):32 * (g % 4) + 32] = L1["maa_w2"][g]
        put(f"maa_w2_{g}", a)
    put("decay_w1", tiles(L1["decay_w1"]))
    put("decay_w2", L1["decay_w2"])
    for n in ("Wr", "Wk", "Wv", "Wg", "Wo"):
        put(n + "T", tiles(L1[n].T))
    for n, m in (("Fk", "ffn_Wk"), ("Fr", "ffn_Wr"), ("Fv", "ffn_Wv")):
        put(n + "T", tiles(L1[m].T))

    V = np.zeros((128, NVEC), np.float32)
    cols = {"ln_q_g": L0["ln_q_g"], "ln_q_b": L0["ln_q_b"], "ln_kv_g": L0["ln_kv_g"], "ln_kv_b": L0["ln_kv_b"],
            "ffn_g": L0["ffn_ln_g"], "ffn_b": L0["ffn_ln_b"], "b1": L0["b1"], "b2": L0["b2"]}
    two = {"ln1_w": "ln1_w", "ln1_b": "ln1_b", "ln2_w": "ln2_w", "ln2_b": "ln2_b", "maa_x": "maa_x", "decay": "time_decay",
           "faaaa": "faaaa", "gn_w": "gn_w", "gn_b": "gn_b", "ffn_k": "ffn_maa_k", "ffn_r": "ffn_maa_r"}
    cols.update({n: L1[m].reshape(-1) for n, m in two.items()})
    cols.update({f"stack{g}": L1["maa_stack"][g] for g in range(5)})
    for n, a in cols.items():
        if a.size == 128:
            V[:, VEC[n]] = a
        else:
            for h in range(2):
                V[:, VEC[f"{n}_{h}"]] = a[h * 128:(h + 1) * 128]

    ang = np.arange(T, dtype=np.float32)[:, None] * np.exp(np.arange(0, C, 2, dtype=np.float32) * np.float32(-math.log(10000.0) / C))
    pos = np.zeros((T, C), np.float32)
    pos[:, 0::2], pos[:, 1::2] = np.sin(ang), np.cos(ang)
    pos = np.ascontiguousarray(pos.T)

    before = f["ctx_2048"][:, 0:2].reshape(B, 2, 2, 128).transpose(0, 3, 2, 1).reshape(B, 128, 4)
    state = f["ctx_2048"][:, 2:2 + S1].reshape(B, 2, 128, S1).transpose(0, 2, 1, 3).reshape(B, 128, 2 * S1)
    first = np.ascontiguousarray(np.concatenate([before, state], axis=2))

    nc = bacc.Bacc("TRN2", target_bir_lowering=False, num_devices=1)
    arrays = {"in_x": np.ascontiguousarray(f["x"]), "in_ctx": np.ascontiguousarray(f["ctx_2048"]), "in_weights": W, "in_vecs": V,
              "in_pos": pos, "in_first": first}
    aps = [nc.dram_tensor(n, a.shape, mybir.dt.from_np(a.dtype), kind="ExternalInput").ap() for n, a in arrays.items()]
    out = nc.dram_tensor("out", (B, NT, E), F32, kind="ExternalOutput").ap()
    build(nc, *aps, out)
    r = run(nc, [arrays], core_ids=[0])
    return r.results[0]["out"]
```
